# Optimizing a Trainium2 kernel written in Bass

```python
import numpy as np
import jax
import jax.numpy as jnp

def _softmax(x, axis=-1):
    return jax.nn.softmax(x, axis=axis)

def _gelu(x):
    return jax.nn.gelu(x, approximate=True)

def _silu(x):
    return jax.nn.silu(x)

def _sigmoid(x):
    return jax.nn.sigmoid(x)

def _layernorm(x, axis=-1, eps=1e-05):
    m = jnp.mean(x, axis=axis, keepdims=True)
    v = jnp.var(x, axis=axis, keepdims=True)
    return (x - m) / jnp.sqrt(v + eps)

def _scatter_add(tgt, idx, src, axis=0):
    return tgt.at[idx].add(src)

def _segment_sum(src, seg, n):
    return jax.ops.segment_sum(src, seg, n)
kernel_name = 'mk_adj_resnorm_d2_adj_r2_7df60a'

def setup_inputs(seed: int=0):
    np.random.seed(seed)
    _w = jnp.asarray

    def _rec_inputs():
        import jax
        import jax.numpy as jnp
        _gk = jax.random.key(seed)
        x = 7.22e-05 + 1 * jax.random.normal(jax.random.fold_in(_gk, 1), (16, 512, 256), jnp.float32)
        _a = jax.random.bernoulli(jax.random.fold_in(_gk, 2), 0.00390625, (16, 512, 512))
        _a = jnp.logical_or(_a, jnp.swapaxes(_a, -1, -2))
        _a = jnp.logical_or(_a, jnp.eye(512, dtype=bool))
        _af = _a.astype(jnp.float32)
        _af = _af * jax.random.uniform(jax.random.fold_in(_gk, 3), (16, 512, 512), jnp.float32, 0.05, 1)
        adj = _af
        return (x, adj)
    x, adj = _rec_inputs()

    def _L0_gnn_setup():
        import jax, jax.numpy as jnp
        import numpy as np
        EPS_LN = 1e-05

        def hypergraph_conv(x, adj, W, b):
            N, C, _ = adj.shape
            H = (adj != 0).astype(x.dtype)
            w = adj.reshape(N, -1)[:, :C]
            xw = jnp.einsum('ncd,hd->nch', x, W)
            Dn = jnp.einsum('nce,ne->nc', H, w)
            Dn = jnp.where(Dn > 0, 1.0 / Dn, 0.0)
            Be = H.sum(axis=1)
            Be = jnp.where(Be > 0, 1.0 / Be, 0.0)
            m = Be[:, :, None] * jnp.einsum('nce,nch->neh', H, xw)
            out = Dn[:, :, None] * jnp.einsum('nce,neh->nch', H, m)
            return out + b

        def layer_norm(x, g, b):
            mu = jnp.mean(x, axis=-1, keepdims=True)
            var = jnp.var(x, axis=-1, keepdims=True)
            return (x - mu) * jax.lax.rsqrt(var + EPS_LN) * g + b
        key = jax.random.key(seed)
        ks = jax.random.split(key, 4)
        N, C, Din, Dh, Dout = (16, 512, 256, 512, 256)
        x = jax.random.normal(ks[0], (N, C, Din), dtype=jnp.float32)
        adj = jax.random.uniform(ks[1], (N, C, C), dtype=jnp.float32, minval=0.1, maxval=1.0)
        W1 = jax.random.normal(ks[2], (Dh, Din), dtype=jnp.float32) * (1.0 / np.sqrt(Din))
        b1 = jnp.zeros((Dh,), dtype=jnp.float32)
        gamma = jnp.ones((Dh,), dtype=jnp.float32)
        beta = jnp.zeros((Dh,), dtype=jnp.float32)
        W2 = jax.random.normal(ks[3], (Dout, Dh), dtype=jnp.float32) * (1.0 / np.sqrt(Dh))
        b2 = jnp.zeros((Dout,), dtype=jnp.float32)
        return {'x': x, 'adj': adj, 'W1': W1, 'b1': b1, 'gamma': gamma, 'beta': beta, 'W2': W2, 'b2': b2}
    _L0_gnn_all = _L0_gnn_setup()
    _L0_gnn_in = {k: v for k, v in _L0_gnn_all.items() if k in ('W1', 'b1', 'gamma', 'beta', 'W2', 'b2')}
    del _L0_gnn_all

    def _L1_gnn_setup():
        import jax, jax.numpy as jnp
        import numpy as np
        B, N, DIN, DOUT, K = (4, 1024, 256, 256, 3)
        key = jax.random.key(seed)
        ks = jax.random.split(key, 8)
        X = jax.random.normal(ks[0], (B, N, DIN), dtype=jnp.float32)
        A = jax.random.uniform(ks[1], (B, N, N), dtype=jnp.float32)
        Wv = jax.random.normal(ks[2], (DIN, DOUT), dtype=jnp.float32) * 0.02
        bv = jax.random.normal(ks[3], (DOUT,), dtype=jnp.float32) * 0.02
        aw = jax.random.normal(ks[4], (2 * DOUT, 1), dtype=jnp.float32) * 0.05
        ab = jax.random.normal(ks[5], (1,), dtype=jnp.float32) * 0.05
        Wk = jax.random.normal(ks[6], (K, DIN, DOUT), dtype=jnp.float32) * 0.02
        bk = jax.random.normal(ks[7], (K, DOUT), dtype=jnp.float32) * 0.02
        return {'X': X, 'A': A, 'Wv': Wv, 'bv': bv, 'aw': aw, 'ab': ab, 'Wk': Wk, 'bk': bk}
    _L1_gnn_all = _L1_gnn_setup()
    _L1_gnn_in = {k: v for k, v in _L1_gnn_all.items() if k in ('Wv', 'bv', 'aw', 'ab', 'Wk', 'bk')}
    del _L1_gnn_all
    return {'x': x, 'adj': adj, 'L0_gnn_W1': _L0_gnn_in['W1'], 'L0_gnn_b1': _L0_gnn_in['b1'], 'L0_gnn_gamma': _L0_gnn_in['gamma'], 'L0_gnn_beta': _L0_gnn_in['beta'], 'L0_gnn_W2': _L0_gnn_in['W2'], 'L0_gnn_b2': _L0_gnn_in['b2'], 'L1_gnn_Wv': _L1_gnn_in['Wv'], 'L1_gnn_bv': _L1_gnn_in['bv'], 'L1_gnn_aw': _L1_gnn_in['aw'], 'L1_gnn_ab': _L1_gnn_in['ab'], 'L1_gnn_Wk': _L1_gnn_in['Wk'], 'L1_gnn_bk': _L1_gnn_in['bk']}

def reference(x, adj, L0_gnn_W1, L0_gnn_b1, L0_gnn_gamma, L0_gnn_beta, L0_gnn_W2, L0_gnn_b2, L1_gnn_Wv, L1_gnn_bv, L1_gnn_aw, L1_gnn_ab, L1_gnn_Wk, L1_gnn_bk):
    import jax
    import jax.numpy as jnp

    def _L0_gnn_ref(x, adj, W1, b1, gamma, beta, W2, b2):
        import jax, jax.numpy as jnp
        import numpy as np
        EPS_LN = 1e-05

        def hypergraph_conv(x, adj, W, b):
            N, C, _ = adj.shape
            H = (adj != 0).astype(x.dtype)
            w = adj.reshape(N, -1)[:, :C]
            xw = jnp.einsum('ncd,hd->nch', x, W)
            Dn = jnp.einsum('nce,ne->nc', H, w)
            Dn = jnp.where(Dn > 0, 1.0 / Dn, 0.0)
            Be = H.sum(axis=1)
            Be = jnp.where(Be > 0, 1.0 / Be, 0.0)
            m = Be[:, :, None] * jnp.einsum('nce,nch->neh', H, xw)
            out = Dn[:, :, None] * jnp.einsum('nce,neh->nch', H, m)
            return out + b

        def layer_norm(x, g, b):
            mu = jnp.mean(x, axis=-1, keepdims=True)
            var = jnp.var(x, axis=-1, keepdims=True)
            return (x - mu) * jax.lax.rsqrt(var + EPS_LN) * g + b
        h = jax.nn.relu(hypergraph_conv(x, adj, W1, b1))
        h = layer_norm(h, gamma, beta)
        y = hypergraph_conv(h, adj, W2, b2)
        return y + x

    def _L1_gnn_ref(X, A, Wv, bv, aw, ab, Wk, bk):
        import jax, jax.numpy as jnp
        import numpy as np
        B, N, DIN, DOUT, K = (4, 1024, 256, 256, 3)
        d = Wv.shape[1]
        Xw = X @ Wv + bv
        sj = Xw @ aw[:d, 0]
        si = Xw @ aw[d:, 0]
        e = jax.nn.leaky_relu(sj[:, None, :] + si[:, :, None] + ab[0], negative_slope=0.2)
        alpha_matrix = A * jnp.exp(e)
        transition = alpha_matrix / (jnp.sum(alpha_matrix, axis=-1, keepdims=True) + 1e-12)
        H = jnp.zeros(X.shape[:-1] + (d,), dtype=X.dtype)
        Xk = X
        for k in range(Wk.shape[0]):
            H = H + Xk @ Wk[k] + bk[k]
            Xk = jnp.einsum('bij,bjd->bid', transition, Xk)
        return jax.nn.relu(H)
    x = _layernorm(x + _L0_gnn_ref(x, adj, L0_gnn_W1, L0_gnn_b1, L0_gnn_gamma, L0_gnn_beta, L0_gnn_W2, L0_gnn_b2), axis=-1)
    x = _layernorm(x + _L1_gnn_ref(x, adj, L1_gnn_Wv, L1_gnn_bv, L1_gnn_aw, L1_gnn_ab, L1_gnn_Wk, L1_gnn_bk), axis=-1)
    return x

_drawn_inputs = setup_inputs


def setup_inputs(seed=0):
    import zlib

    import numpy as np

    out = dict(_drawn_inputs(seed))
    spreads = {'L0_gnn_b1': (0.0, 0.1),
     'L0_gnn_gamma': (1.0, 0.2),
     'L0_gnn_beta': (0.0, 0.303),
     'L0_gnn_b2': (0.0, 0.1)}
    factors = {'L1_gnn_Wv': 2.891, 'L1_gnn_bv': 21.606, 'L1_gnn_aw': 2.852}
    for name, (base, spread) in spreads.items():
        noise = np.random.default_rng([zlib.crc32(name.encode()), seed]).standard_normal(out[name].shape)
        drawn = base * np.exp(spread * noise) if base else spread * noise
        out[name] = jnp.asarray(drawn.astype(out[name].dtype))
    for name, factor in factors.items():
        out[name] = (out[name] * factor).astype(out[name].dtype)
    return out
```

```python
import numpy as np
import concourse.bass as bass
from concourse import mybir
from contextlib import ExitStack


def resnorm_hypergraph_attention_kernel(
    nc: bass.Bass,
    x: bass.AP,
    adj: bass.AP,
    W1: bass.AP,
    b1: bass.AP,
    gamma: bass.AP,
    beta: bass.AP,
    W2: bass.AP,
    b2: bass.AP,
    Wv: bass.AP,
    bv: bass.AP,
    aw: bass.AP,
    ab: bass.AP,
    Wk: bass.AP,
    bk: bass.AP,
    out: bass.AP,
):
    f32 = mybir.dt.float32
    f32r = mybir.dt.float32r
    ALU = mybir.AluOpType
    ACT = mybir.ActivationFunctionType
    AX = mybir.AxisListType

    P = 128
    B, C, D = x.shape
    HID = W1.shape[0]
    K = Wk.shape[0]
    NT, DT, HT = C // P, D // P, HID // P
    DE = D + 2
    LN_EPS = 1e-5
    ROW_EPS = 1e-12
    SLOPE = 0.2
    SMALLEST = float(np.finfo(np.float32).tiny)
    assert K == 3 and NT == 4 and DT == 2 and HT == 4

    ctx = ExitStack()
    with ctx:
        def sb(name, shape, dt=f32):
            return ctx.enter_context(nc.sbuf_tensor(name, shape, dt))

        def sem(name):
            return ctx.enter_context(nc.semaphore(name))

        ident = sb("ident", [P, P])
        ones2 = sb("ones2", [P, 2], f32r)
        minus_half = sb("minus_half", [P, NT])
        w1_hi = sb("w1_hi", [P, DT, HID], f32r)
        w1_lo = sb("w1_lo", [P, DT, HID], f32r)
        w2_hi = sb("w2_hi", [P, HT, DE], f32r)
        w2_lo = sb("w2_lo", [P, HT, D], f32r)
        wk2_hi = sb("wk2_hi", [P, DT, D + 4], f32r)
        wk2_lo = sb("wk2_lo", [P, DT, D + 4], f32r)
        wk10_hi = sb("wk10_hi", [P, DT, 2 * D], f32r)
        wk10_lo = sb("wk10_lo", [P, DT, 2 * D], f32r)
        b1_col = sb("b1_col", [P, HT])
        gamma_col = sb("gamma_col", [P, HT])
        beta_col = sb("beta_col", [P, HT])
        beta_row = sb("beta_row", [P, D])
        b2_row = sb("b2_row", [P, D])
        bk_row = sb("bk_row", [P, D])
        score_dots = sb("score_dots", [P, 4])
        wv_dots = sb("wv_dots", [P, DT, 2])

        adj_sb = sb("adj_sb", [P, NT, C])
        inc = sb("inc", [P, NT, C], f32r)
        incT = sb("incT", [P, NT, C], f32r)
        adjT = sb("adjT", [P, 2, NT, C])
        x_sb = sb("x_sb", [P, NT, D])
        node_hi = sb("node_hi", [P, NT, DE], f32r)
        node_lo = sb("node_lo", [P, NT, D], f32r)
        edge_hi = sb("edge_hi", [P, NT, DE], f32r)
        edge_lo = sb("edge_lo", [P, NT, D], f32r)
        resid = sb("resid", [P, NT, D])
        mix = sb("mix", [P, NT, D])
        turn_hi = sb("turn_hi", [P, DT * C], f32r)
        turn_lo = sb("turn_lo", [P, DT * C], f32r)
        hid = sb("hid", [P, HT, C])
        hid_hi = sb("hid_hi", [P, HT, C], f32r)
        hid_lo = sb("hid_lo", [P, HT, C], f32r)
        square = sb("square", [P, 2, C])
        square_sum = sb("square_sum", [P, C])
        square_hi = sb("square_hi", [P, C], f32r)
        square_lo = sb("square_lo", [P, C], f32r)

        X_pair = sb("X_pair", [P, 2, NT, D])
        X = X_pair[:, 0, :, :]
        X_kept = X_pair[:, 1, :, :]
        XT_hi = sb("XT_hi", [P, DT, C], f32r)
        XT_lo = sb("XT_lo", [P, DT, C], f32r)
        expo = sb("expo", [P, NT, C])
        expo_slope = sb("expo_slope", [P, 2, C])
        att_hi = sb("att_hi", [P, NT, C], f32r)
        att_lo = sb("att_lo", [P, NT, C], f32r)
        z2_hi = sb("z2_hi", [P, NT, DE], f32r)
        z2_lo = sb("z2_lo", [P, NT, D], f32r)
        z1 = sb("z1", [P, NT, D])
        z0 = sb("z0", [P, NT, D])
        out_sb = sb("out_sb", [P, NT, D])

        nodes_of = sb("nodes_of", [P, NT])
        Be = sb("Be", [P, NT])
        D_sum = sb("D_sum", [P, NT])
        D_safe = sb("D_safe", [P, NT])
        D_inv = sb("D_inv", [P, NT])
        Dn = sb("Dn", [P, NT])
        hid_mean = sb("hid_mean", [P, NT])
        hid_mean2 = sb("hid_mean2", [P, NT])
        hid_var = sb("hid_var", [P, NT])
        hid_var_eps = sb("hid_var_eps", [P, NT])
        hid_rstd = sb("hid_rstd", [P, NT])
        stats0 = sb("stats0", [P, NT, 6])
        mean_sum0 = sb("mean_sum0", [P, NT])
        mean_gap0 = sb("mean_gap0", [P, NT])
        square_dev0 = sb("square_dev0", [P, NT])
        gap_square0 = sb("gap_square0", [P, NT])
        mean0 = sb("mean0", [P, NT])
        var_eps0 = sb("var_eps0", [P, NT])
        rstd0 = sb("rstd0", [P, NT])
        score_i = sb("score_i", [P, NT])
        bias_j = sb("bias_j", [P, NT])
        bias_j_slope = sb("bias_j_slope", [P, NT])
        row_sum = sb("row_sum", [P, NT])
        row_inv = sb("row_inv", [P, NT])
        stats1 = sb("stats1", [P, NT, 6])
        mean_sum1 = sb("mean_sum1", [P, NT])
        mean_gap1 = sb("mean_gap1", [P, NT])
        square_dev1 = sb("square_dev1", [P, NT])
        gap_square1 = sb("gap_square1", [P, NT])
        shift1 = sb("shift1", [P, NT])
        neg_mean1 = sb("neg_mean1", [P, NT])
        var_eps1 = sb("var_eps1", [P, NT])
        rstd1 = sb("rstd1", [P, NT])

        w1_raw = adjT[:, 0, 0:2, :].rearrange("p a n -> p (a n)").rearrange("p (t d) -> p t d", d=D)
        w2_raw = adjT[:, 1, 0:2, :]
        wk_raw = X_pair[:, :, :, :].rearrange("p a t d -> p (a t) d")
        wv_raw = z1[:, 0:DT, :]
        aw_row = z0[:, 0:2, :]
        bv_row = z0[:, 2, :]
        dot_tmp = z0[:, 3, :]
        bk_raw = z1[:, 2:4, :]
        bk_raw2 = expo[:, 0, 0:D]
        wv_tmp = expo[:, 1, 0:D]
        w2_gamma = hid[:, 0:2, :].rearrange("p a n -> p (a n)").rearrange("p (t d) -> p t d", d=D)
        w2_plain = hid[:, 2:4, :].rearrange("p a n -> p (a n)").rearrange("p (t d) -> p t d", d=D)
        beta_wide = square[:, 0, :].rearrange("p (t n) -> p t n", n=P)
        ones_wide = square[:, 1, 0:P]

        ps = ctx.enter_context(nc.psum_tensor("ps", [P, 8, 512], f32))
        T_BANKS = [6, 7, 0, 1]
        XT_BANKS = [4, 5]
        TURN_BANKS = [0, 1]
        W1_BANKS = [4, 5, 6, 7]
        SI_BANK = 3
        SQ_BANK, SQ_COL = 7, D + 8
        Z10_BANKS = [2, 0, 1, 3]

        def half(bank0, t):
            return ps[:, bank0 + t // 2, (t % 2) * D:(t % 2 + 1) * D]

        weights_loaded = sem("weights_loaded")
        rows_loaded = sem("rows_loaded")
        adj_loaded = sem("adj_loaded")
        x_loaded = sem("x_loaded")
        out_stored = sem("out_stored")
        ident_ready = sem("ident_ready")
        gp_consts = sem("gp_consts")
        setup_pe = sem("setup_pe")
        setup_act = sem("setup_act")
        setup_dve = sem("setup_dve")
        adjT_psum = sem("adjT_psum")
        gather1_psum = sem("gather1_psum")
        scatter1_psum = sem("scatter1_psum")
        turn_psum = sem("turn_psum")
        hid_psum = sem("hid_psum")
        w2_psum = sem("w2_psum")
        square_psum = sem("square_psum")
        gather2_psum = sem("gather2_psum")
        scatter2_psum = sem("scatter2_psum")
        XT_psum = sem("XT_psum")
        z2_psum = sem("z2_psum")
        si_psum = sem("si_psum")
        z10_psum = sem("z10_psum")
        hop1_psum = sem("hop1_psum")
        hop2_psum = sem("hop2_psum")
        inc_ready = sem("inc_ready")
        incT_ready = sem("incT_ready")
        adjT_ready = sem("adjT_ready")
        w_hi_ready = sem("w_hi_ready")
        w_ready = sem("w_ready")
        x_hi_ready = sem("x_hi_ready")
        x_lo_ready = sem("x_lo_ready")
        twice_x = sem("twice_x")
        resid_ready = sem("resid_ready")
        nodes_counted = sem("nodes_counted")
        Be_ready = sem("Be_ready")
        edge_hi_ready = sem("edge_hi_ready")
        edge_lo_ready = sem("edge_lo_ready")
        D_summed = sem("D_summed")
        D_clamped = sem("D_clamped")
        D_inverted = sem("D_inverted")
        Dn_ready = sem("Dn_ready")
        mix_scaled = sem("mix_scaled")
        turn_hi_ready = sem("turn_hi_ready")
        turn_lo_ready = sem("turn_lo_ready")
        hid_ready = sem("hid_ready")
        hid_hi_ready = sem("hid_hi_ready")
        hid_lo_ready = sem("hid_lo_ready")
        squared = sem("squared")
        squares_added = sem("squares_added")
        square_hi_ready = sem("square_hi_ready")
        square_lo_ready = sem("square_lo_ready")
        hid_stats = sem("hid_stats")
        hid_rstd_ready = sem("hid_rstd_ready")
        y_ready = sem("y_ready")
        y_hi_ready = sem("y_hi_ready")
        y_lo_ready = sem("y_lo_ready")
        sum_ready = sem("sum_ready")
        sum_stats = sem("sum_stats")
        sum_moments = sem("sum_moments")
        rstd0_ready = sem("rstd0_ready")
        X_ready = sem("X_ready")
        X_copied = sem("X_copied")
        XT_hi_ready = sem("XT_hi_ready")
        XT_lo_ready = sem("XT_lo_ready")
        bias_j_ready = sem("bias_j_ready")
        score_i_ready = sem("score_i_ready")
        z2_hi_ready = sem("z2_hi_ready")
        z2_lo_ready = sem("z2_lo_ready")
        exp_ready = sem("exp_ready")
        exp_slope_ready = sem("exp_slope_ready")
        exp_larger = sem("exp_larger")
        att_ready = sem("att_ready")
        att_hi_ready = sem("att_hi_ready")
        att_lo_ready = sem("att_lo_ready")
        z1_ready = sem("z1_ready")
        z0_ready = sem("z0_ready")
        rows_summed = sem("rows_summed")
        row_inv_ready = sem("row_inv_ready")
        hop_ready = sem("hop_ready")
        hop_hi_ready = sem("hop_hi_ready")
        hop_lo_ready = sem("hop_lo_ready")
        hop2_added = sem("hop2_added")
        relu_added = sem("relu_added")
        out_stats = sem("out_stats")
        out_moments = sem("out_moments")
        rstd1_ready = sem("rstd1_ready")
        shift1_ready = sem("shift1_ready")
        out_ready = sem("out_ready")

        def wait(eng, semaphore, count):
            if not isinstance(count, int) or count > 0:
                eng.wait_ge(semaphore, count)

        def samples(eng, layer0, body, finish):
            layer0()
            body(0, False, True, True)
            with eng.Fori(1, B - 2) as r:
                body(r, True, True, True)
            body(B - 2, True, True, False)
            body(B - 1, True, False, False)
            finish(B - 1)

        SETUP_GAMMA = 4 + 1 + DT + HT
        SETUP_DONE = SETUP_GAMMA + 6 + 8 + 4 + 1 + 2 + 3 + 1 + HT + 1 + 1 + 1

        block = ctx.enter_context(nc.Block())

        @block.sync
        def _(eng):
            eng.dma_start(w1_raw, W1.rearrange("(t p) d -> p t d", p=P)).then_inc(weights_loaded, 16)
            eng.dma_start(w2_raw, W2.rearrange("(t p) h -> p t h", p=P)).then_inc(weights_loaded, 16)

            def load_adj(s):
                wait(eng, inc_ready, s)
                wait(eng, adjT_psum, 4 * s)
                eng.dma_start(adj_sb[:, :, :], adj[s].rearrange("(t p) e -> p t e", p=P)).then_inc(adj_loaded, 16)

            def load_x(s):
                wait(eng, x_lo_ready, s)
                wait(eng, twice_x, s)
                eng.dma_start(x_sb[:, :, :], x[s].rearrange("(t p) d -> p t d", p=P)).then_inc(x_loaded, 16)

            def store_out(r):
                eng.wait_ge(out_ready, 4 * (r + 1))
                eng.dma_start(out[r].rearrange("(t p) d -> p t d", p=P), out_sb[:, :, :]).then_inc(out_stored, 16)

            def layer0():
                load_adj(0)
                load_x(0)
                for i, v in enumerate((gamma, beta, b1)):
                    eng.dma_start((gamma_col, beta_col, b1_col)[i][:, :],
                                  v.rearrange("(t p) -> p t", p=P), allow_slow_non_contiguous=True).then_inc(weights_loaded, 16)
                load_adj(1)

            def addresses(r):
                if not isinstance(r, int):
                    eng.compute_val(4 * (r + 2))
                    eng.compute_val((r + 1) * (C * D) * 4)
                    eng.compute_val((r + 2) * (C * C) * 4)
                    eng.compute_val((r - 1) * (C * D) * 4)

            def body(r, last_hop, first_layer, prepare):
                addresses(r)
                if first_layer:
                    load_x(r + 1)
                if prepare:
                    load_adj(r + 2)
                if last_hop:
                    store_out(r - 1)

            def finish(r):
                store_out(r)

            samples(eng, layer0, body, finish)
            eng.wait_ge(out_stored, 16 * B)

        @block.gpsimd
        def _(eng):
            eng.memset(ident[:, :], 0.0).then_inc(ident_ready, 1)
            eng.wait_ge(ident_ready, 1)
            eng.affine_select(out=ident[:, :], in_=ident[:, :], compare_op=ALU.not_equal, fill=1.0,
                              base=0, pattern=[[-1, P]], channel_multiplier=1).then_inc(ident_ready, 1)
            eng.memset(ones_wide, 1.0).then_inc(gp_consts, 1)
            eng.memset(minus_half[:, :], -0.5).then_inc(gp_consts, 1)

            def double_x(s):
                eng.wait_ge(x_loaded, 16 * (s + 1))
                wait(eng, X_ready, 4 * s)
                eng.tensor_tensor(resid[:, :, :], x_sb[:, :, :], x_sb[:, :, :], ALU.add).then_inc(twice_x, 1)
                eng.wait_ge(twice_x, s + 1)
                for t in range(NT):
                    eng.tensor_tensor(resid[:, t, :], resid[:, t, :], b2_row[:, :], ALU.add).then_inc(resid_ready, 1)

            def power_out(r):
                eng.wait_ge(out_moments, 6 * (r + 1))
                wait(eng, out_ready, 4 * r)
                eng.tensor_tensor(rstd1[:, :], var_eps1[:, :], minus_half[:, :], ALU.pow).then_inc(rstd1_ready, 1)
                eng.wait_ge(rstd1_ready, r + 1)
                eng.tensor_tensor(shift1[:, :], neg_mean1[:, :], rstd1[:, :], ALU.mult).then_inc(shift1_ready, 1)

            def weigh_attention(r):
                eng.wait_ge(adjT_ready, 4 * (r + 1))
                for j in range(NT):
                    eng.wait_ge(exp_larger, 4 * r + j + 1)
                    eng.tensor_tensor(expo[:, j, :], expo[:, j, :], adjT[:, r % 2, j, :],
                                      ALU.mult).then_inc(att_ready, 1)

            def add_squares(s):
                eng.wait_ge(squared, 4 * s + 2)
                wait(eng, square_lo_ready, s)
                eng.tensor_tensor(square_sum[:, :], square[:, 0, :], square[:, 1, :], ALU.add).then_inc(squares_added, 1)
                for t in range(2, HT):
                    eng.wait_ge(squared, 4 * s + t + 1)
                    eng.wait_ge(squares_added, 3 * s + t - 1)
                    eng.tensor_tensor(square_sum[:, :], square_sum[:, :], square[:, t % 2, :],
                                      ALU.add).then_inc(squares_added, 1)

            def power_hidden(s):
                eng.wait_ge(hid_stats, 4 * (s + 1))
                eng.tensor_tensor(hid_rstd[:, :], hid_var_eps[:, :], minus_half[:, :], ALU.pow).then_inc(hid_rstd_ready, 1)

            def power_sum(s):
                eng.wait_ge(sum_moments, 6 * (s + 1))
                eng.tensor_tensor(rstd0[:, :], var_eps0[:, :], minus_half[:, :], ALU.pow).then_inc(rstd0_ready, 1)

            def layer0():
                eng.wait_ge(gp_consts, 2)
                eng.wait_ge(rows_loaded, 16 * 9)
                double_x(0)
                add_squares(0)
                power_hidden(0)
                power_sum(0)

            def body(r, last_hop, first_layer, prepare):
                s = r + 1
                if first_layer:
                    double_x(s)
                weigh_attention(r)
                if last_hop:
                    power_out(r - 1)
                if first_layer:
                    add_squares(s)
                if first_layer:
                    power_hidden(s)
                    power_sum(s)

            samples(eng, layer0, body, power_out)

        @block.scalar
        def _(eng):
            eng.dma_start(wk_raw[:, 0:K * DT, :], Wk.rearrange("k (t p) o -> p (k t) o", p=P)).then_inc(rows_loaded, 16)
            eng.dma_start(wv_raw, Wv.rearrange("(t p) o -> p t o", p=P)).then_inc(rows_loaded, 16)
            eng.dma_start(aw_row, aw.rearrange("(a n) b -> b a n", a=2).to_broadcast([P, 2, D])).then_inc(rows_loaded, 16)
            eng.dma_start(bv_row, bv.rearrange("(a n) -> a n", a=1).to_broadcast([P, D])).then_inc(rows_loaded, 16)
            eng.dma_start(score_dots[:, 2:3], ab.rearrange("(a n) -> a n", a=1).to_broadcast([P, 1])).then_inc(rows_loaded, 16)
            eng.dma_start(bk_raw[:, 0, :], bk[0:1, :].to_broadcast([P, D])).then_inc(rows_loaded, 16)
            eng.dma_start(bk_raw[:, 1, :], bk[1:2, :].to_broadcast([P, D])).then_inc(rows_loaded, 16)
            eng.dma_start(bk_raw2, bk[2:3, :].to_broadcast([P, D])).then_inc(rows_loaded, 16)
            eng.dma_start(b2_row[:, :], b2.rearrange("(a n) -> a n", a=1).to_broadcast([P, D])).then_inc(rows_loaded, 16)

            for d in range(DT):
                eng.wait_ge(setup_pe, d + 1)
                eng.activation(w1_hi[:, d, :], ps[:, d, :], ACT.Copy).then_inc(setup_act, 1)
            for t in range(HT):
                eng.wait_ge(setup_pe, DT + t + 1)
                eng.activation(w2_plain[:, t, :], ps[:, 2 + t, 0:D], ACT.Copy).then_inc(setup_act, 1)

            def split_edges(s, conv):
                eng.wait_ge(Be_ready, s + 1)
                wait(eng, scatter2_psum if conv == 0 else scatter1_psum, 2 * s if conv == 0 else 4 * (s + 1))
                for t in range(NT):
                    if conv == 0:
                        src = ps[:, t, 0:D]
                    else:
                        eng.wait_ge(gather2_psum, 2 * s + t // 2 + 1)
                        src = half(4, t)
                    eng.activation(edge_hi[:, t, 0:D], src, ACT.Copy, scale=Be[:, t:t + 1]).then_inc(edge_hi_ready, 1)

            def split_XT(r):
                wait(eng, z10_psum, 4 * r)
                for d in range(DT):
                    eng.wait_ge(XT_psum, 2 * r + d + 1)
                    eng.activation(XT_hi[:, d, :], ps[:, XT_BANKS[d], :], ACT.Copy).then_inc(XT_hi_ready, 1)

            def keep_X(r):
                eng.wait_ge(X_ready, 4 * (r + 1))
                wait(eng, relu_added, r)
                eng.activation(X_kept, X, ACT.Copy).then_inc(X_copied, 1)

            def normalise_out(r):
                eng.wait_ge(shift1_ready, r + 1)
                wait(eng, out_stored, 16 * r)
                for t in range(NT):
                    eng.activation(out_sb[:, t, :], z0[:, t, :], ACT.Identity, bias=shift1[:, t:t + 1],
                                   scale=rstd1[:, t:t + 1]).then_inc(out_ready, 1)

            def scale_mix(s):
                eng.wait_ge(Dn_ready, s + 1)
                wait(eng, y_lo_ready, 4 * s)
                for t in range(NT):
                    eng.activation(mix[:, t, :], ps[:, t, 0:D], ACT.Copy, scale=Dn[:, t:t + 1]).then_inc(mix_scaled, 1)

            def split_z2(r):
                eng.wait_ge(bias_j_ready, 2 * (r + 1))
                wait(eng, hop1_psum, 4 * r)
                for t in range(NT):
                    eng.activation(z2_hi[:, t, 0:D], ps[:, 4 + t, 0:D], ACT.Copy).then_inc(z2_hi_ready, 1)

            def exponentials(r, j):
                if j == 0:
                    eng.wait_ge(si_psum, r + 1)
                if j < 2:
                    wait(eng, exp_larger, 4 * r)
                else:
                    eng.wait_ge(exp_larger, 4 * r + j - 1)
                if j == 0:
                    wait(eng, att_lo_ready, 4 * r)
                eng.activation(expo[:, j, :], ps[:, SI_BANK, :], ACT.Exp,
                               bias=bias_j[:, j:j + 1]).then_inc(exp_ready, 1)
                eng.activation(expo_slope[:, j % 2, :], ps[:, SI_BANK, :], ACT.Exp,
                               bias=bias_j_slope[:, j:j + 1], scale=SLOPE).then_inc(exp_slope_ready, 1)

            def split_attention(r, j):
                if j == 0:
                    wait(eng, hop2_psum, 2 * r)
                eng.wait_ge(att_ready, 4 * r + j + 1)
                eng.activation(att_hi[:, j, :], expo[:, j, :], ACT.Copy).then_inc(att_hi_ready, 1)

            def split_turn(s):
                wait(eng, hop2_psum, 2 * (s - 1))
                for d in range(DT):
                    eng.wait_ge(turn_psum, 2 * s + d + 1)
                    eng.activation(turn_hi[:, d * C:(d + 1) * C], ps[:, TURN_BANKS[d], :],
                                   ACT.Copy).then_inc(turn_hi_ready, 1)

            def copy_z1(r, t):
                eng.wait_ge(z10_psum, 4 * r + t + 1)
                if t == 0:
                    wait(eng, hop_lo_ready, 4 * r)
                eng.activation(z1[:, t, :], ps[:, Z10_BANKS[t], 0:D], ACT.Copy).then_inc(z1_ready, 1)

            def hidden(s):
                wait(eng, hid_lo_ready, 4 * s)
                for t in range(HT):
                    eng.wait_ge(hid_psum, 4 * s + t + 1)
                    eng.activation(hid[:, t, :], ps[:, W1_BANKS[t], :], ACT.Relu,
                                   bias=b1_col[:, t:t + 1]).then_inc(hid_ready, 1)

            def squares(s, tiles):
                for t in tiles:
                    eng.wait_ge(hid_ready, 4 * s + t + 1)
                    if t >= 2:
                        eng.wait_ge(squares_added, 3 * s + 1)
                    else:
                        wait(eng, squares_added, 3 * s)
                    eng.activation(square[:, t % 2, :], hid[:, t, :], ACT.Square).then_inc(squared, 1)

            def split_y(s):
                for t in range(NT):
                    eng.wait_ge(y_ready, 4 * s + t + 1)
                    eng.activation(node_hi[:, t, 0:D], mix[:, t, :], ACT.Copy).then_inc(y_hi_ready, 1)

            def split_hop(r):
                for t in range(NT):
                    eng.wait_ge(hop_ready, 4 * r + t + 1)
                    eng.activation(turn_hi[:, t * D:(t + 1) * D], z1[:, t, :], ACT.Copy).then_inc(hop_hi_ready, 1)

            def copy_adjT(s):
                wait(eng, att_ready, 4 * (s - 1))
                for t in range(NT):
                    eng.wait_ge(adjT_psum, 4 * s + t + 1)
                    eng.activation(adjT[:, s % 2, t, :], ps[:, T_BANKS[t], :], ACT.Copy).then_inc(adjT_ready, 1)

            def layer0():
                copy_adjT(0)
                split_edges(0, 0)
                scale_mix(0)
                split_turn(0)
                hidden(0)
                squares(0, range(HT))
                split_y(0)
                split_edges(0, 1)
                copy_adjT(1)

            def body(r, last_hop, first_layer, prepare):
                s = r + 1
                if first_layer:
                    split_edges(s, 0)
                split_XT(r)
                if first_layer:
                    scale_mix(s)
                split_z2(r)
                if first_layer:
                    split_turn(s)
                for j in range(NT):
                    exponentials(r, j)
                if first_layer:
                    hidden(s)
                    squares(s, (0, 1))
                split_attention(r, 0)
                copy_z1(r, 0)
                split_attention(r, 1)
                copy_z1(r, 1)
                if first_layer:
                    squares(s, (2, 3))
                split_attention(r, 2)
                split_attention(r, 3)
                copy_z1(r, 2)
                if last_hop:
                    normalise_out(r - 1)
                copy_z1(r, 3)
                keep_X(r)
                if first_layer:
                    split_y(s)
                split_hop(r)
                if first_layer:
                    split_edges(s, 1)
                if prepare:
                    copy_adjT(s + 1)

            samples(eng, layer0, body, normalise_out)

        @block.vector
        def _(eng):
            def low(dst, src, high, done):
                eng.tensor_tensor(dst, src, high.bitcast(f32), ALU.subtract).then_inc(done, 1)

            eng.memset(ones2[:, :].bitcast(f32), 1.0).then_inc(setup_dve, 1)
            eng.memset(node_hi[:, :, D:DE].bitcast(f32), 1.0).then_inc(setup_dve, 1)
            eng.memset(z2_hi[:, :, D:DE].bitcast(f32), 1.0).then_inc(setup_dve, 1)
            eng.memset(w2_hi[:, :, D:DE].bitcast(f32), 1.0).then_inc(setup_dve, 1)

            def setup():
                done = 4
                eng.wait_ge(weights_loaded, 16 * 5)
                eng.tensor_copy(beta_wide, beta_col[:, :].unsqueeze(2).to_broadcast([P, HT, P])).then_inc(setup_dve, 1)
                done += 1
                for d in range(DT):
                    eng.wait_ge(setup_act, d + 1)
                    low(w1_lo[:, d, :], ps[:, d, :], w1_hi[:, d, :], setup_dve)
                    done += 1
                for t in range(HT):
                    eng.wait_ge(setup_act, DT + t + 1)
                    eng.tensor_scalar(w2_gamma[:, t, :], ps[:, 2 + t, 0:D], gamma_col[:, t:t + 1], None,
                                      ALU.mult).then_inc(setup_dve, 1)
                    done += 1
                gamma_done = done
                eng.wait_ge(rows_loaded, 16 * 9)
                for hi, lo, k, c0 in ((wk2_hi, wk2_lo, 2, 0), (wk10_hi, wk10_lo, 1, 0), (wk10_hi, wk10_lo, 0, D)):
                    raw = wk_raw[:, k * DT:(k + 1) * DT, :]
                    eng.tensor_copy(hi[:, :, c0:c0 + D], raw).then_inc(setup_dve, 1)
                    done += 1
                    eng.wait_ge(setup_dve, done)
                    low(lo[:, :, c0:c0 + D], raw, hi[:, :, c0:c0 + D], setup_dve)
                    done += 1
                for d in range(DT):
                    for a in range(2):
                        eng.tensor_tensor(wv_tmp, wv_raw[:, d, :], aw_row[:, a, :], ALU.mult).then_inc(setup_dve, 1)
                        done += 1
                        eng.wait_ge(setup_dve, done)
                        eng.reduce_sum(wv_dots[:, d, a:a + 1], wv_tmp, axis=AX.X).then_inc(setup_dve, 1)
                        done += 1
                        eng.wait_ge(setup_dve, done)
                for a in range(2):
                    eng.tensor_tensor(dot_tmp, bv_row, aw_row[:, a, :], ALU.mult).then_inc(setup_dve, 1)
                    done += 1
                    eng.wait_ge(setup_dve, done)
                    eng.reduce_sum(score_dots[:, a:a + 1], dot_tmp, axis=AX.X).then_inc(setup_dve, 1)
                    done += 1
                    eng.wait_ge(setup_dve, done)
                eng.reduce_sum(score_dots[:, 3:4], score_dots[:, 0:3], axis=AX.X).then_inc(setup_dve, 1)
                done += 1
                for a in range(2):
                    v = wv_dots[:, :, a:a + 1].to_broadcast([P, DT, 2])
                    c0 = D + 2 * a
                    eng.tensor_copy(wk2_hi[:, :, c0:c0 + 2], v).then_inc(setup_dve, 1)
                    done += 1
                    eng.wait_ge(setup_dve, done)
                    low(wk2_lo[:, :, c0:c0 + 2], v, wk2_hi[:, :, c0:c0 + 2], setup_dve)
                    done += 1
                eng.tensor_tensor(bk_row[:, :], bk_raw[:, 0, :], bk_raw[:, 1, :], ALU.add).then_inc(setup_dve, 1)
                done += 1
                eng.wait_ge(setup_dve, done)
                eng.tensor_tensor(bk_row[:, :], bk_row[:, :], bk_raw2, ALU.add).then_inc(setup_dve, 1)
                done += 1
                eng.wait_ge(setup_pe, DT + HT + 2)
                for t in range(HT):
                    eng.scalar_tensor_tensor(w2_gamma[:, t, :], ps[:, 6, 0:D], -1.0 / HID, w2_gamma[:, t, :],
                                             ALU.mult, ALU.add).then_inc(setup_dve, 1)
                    done += 1
                eng.tensor_copy(beta_row[:, :], ps[:, 7, 0:D]).then_inc(setup_dve, 1)
                done += 1
                eng.wait_ge(setup_dve, done)
                eng.tensor_copy(w2_hi[:, :, 0:D], w2_gamma).then_inc(setup_dve, 1)
                done += 1
                eng.wait_ge(setup_dve, done)
                low(w2_lo[:, :, :], w2_gamma, w2_hi[:, :, 0:D], setup_dve)
                done += 1
                assert gamma_done == SETUP_GAMMA and done == SETUP_DONE
                eng.wait_ge(setup_dve, done)

            def split_input(s):
                eng.wait_ge(adj_loaded, 16 * (s + 1))
                wait(eng, gather2_psum, 2 * s)
                eng.tensor_scalar(inc[:, :, :], adj_sb[:, :, :], 0.0, None, ALU.not_equal).then_inc(inc_ready, 1)
                eng.wait_ge(x_loaded, 16 * (s + 1))
                eng.tensor_copy(node_hi[:, :, 0:D], x_sb[:, :, :]).then_inc(x_hi_ready, 1)
                eng.wait_ge(x_hi_ready, s + 1)
                low(node_lo[:, :, :], x_sb[:, :, :], node_hi[:, :, 0:D], x_lo_ready)

            def transpose_incidence(s):
                eng.wait_ge(adjT_ready, 4 * (s + 1))
                wait(eng, scatter2_psum, 2 * s)
                wait(eng, scatter1_psum, 4 * s)
                eng.tensor_scalar(incT[:, :, :], adjT[:, s % 2, :, :], 0.0, None, ALU.not_equal).then_inc(incT_ready, 1)
                w_col = adjT[:, s % 2, :, 0:1]
                eng.tensor_copy(edge_hi[:, :, D:D + 1], w_col).then_inc(w_hi_ready, 1)
                eng.wait_ge(w_hi_ready, s + 1)
                low(edge_hi[:, :, D + 1:DE], w_col, edge_hi[:, :, D:D + 1], w_ready)

            def edges(s):
                eng.wait_ge(gather1_psum, 4 * (s + 1))
                eng.tensor_scalar(nodes_of[:, :], ps[:, 0:NT, D], 1.0, None, ALU.max).then_inc(nodes_counted, 1)
                eng.wait_ge(nodes_counted, s + 1)
                eng.reciprocal(Be[:, :], nodes_of[:, :]).then_inc(Be_ready, 1)
                for t in range(NT):
                    eng.wait_ge(edge_hi_ready, 8 * s + t + 1)
                    eng.scalar_tensor_tensor(edge_lo[:, t, :], ps[:, t, 0:D], Be[:, t:t + 1],
                                             edge_hi[:, t, 0:D].bitcast(f32), ALU.mult, ALU.subtract)\
                       .then_inc(edge_lo_ready, 1)

            def edges2(s):
                for t in range(NT):
                    eng.wait_ge(edge_hi_ready, 8 * s + 4 + 2 * (t // 2) + 2)
                    eng.scalar_tensor_tensor(edge_lo[:, t, :], half(4, t), Be[:, t:t + 1],
                                             edge_hi[:, t, 0:D].bitcast(f32), ALU.mult, ALU.subtract)\
                       .then_inc(edge_lo_ready, 1)

            def degrees(s):
                eng.wait_ge(scatter1_psum, 4 * (s + 1))
                eng.reduce_sum(D_sum[:, :], ps[:, 0:NT, D:DE], axis=AX.X).then_inc(D_summed, 1)
                eng.wait_ge(D_summed, s + 1)
                eng.tensor_scalar(D_safe[:, :], D_sum[:, :], SMALLEST, None, ALU.max).then_inc(D_clamped, 1)
                eng.wait_ge(D_clamped, s + 1)
                eng.reciprocal(D_inv[:, :], D_safe[:, :]).then_inc(D_inverted, 1)
                eng.wait_ge(D_inverted, s + 1)
                eng.scalar_tensor_tensor(Dn[:, :], D_sum[:, :], 0.0, D_inv[:, :], ALU.is_gt, ALU.mult)\
                   .then_inc(Dn_ready, 1)

            def turn_low(s):
                for d in range(DT):
                    eng.wait_ge(turn_hi_ready, 2 * s + d + 1)
                    low(turn_lo[:, d * C:(d + 1) * C], ps[:, TURN_BANKS[d], :], turn_hi[:, d * C:(d + 1) * C],
                        turn_lo_ready)

            def split_hidden(s):
                wait(eng, w2_psum, 4 * s)
                for t in range(HT):
                    eng.wait_ge(hid_ready, 4 * s + t + 1)
                    eng.tensor_copy(hid_hi[:, t, :], hid[:, t, :]).then_inc(hid_hi_ready, 1)
                    eng.wait_ge(hid_hi_ready, 4 * s + t + 1)
                    low(hid_lo[:, t, :], hid[:, t, :], hid_hi[:, t, :], hid_lo_ready)

            def split_squares(s):
                eng.wait_ge(squares_added, 3 * (s + 1))
                wait(eng, square_psum, s)
                eng.tensor_copy(square_hi[:, :], square_sum[:, :]).then_inc(square_hi_ready, 1)
                eng.wait_ge(square_hi_ready, s + 1)
                low(square_lo[:, :], square_sum[:, :], square_hi[:, :], square_lo_ready)

            def hidden_norm(s):
                eng.wait_ge(square_psum, s + 1)
                eng.tensor_scalar(hid_mean[:, :], ps[:, 4:4 + NT, D], 1.0 / HID, None, ALU.mult).then_inc(hid_stats, 1)
                eng.wait_ge(hid_stats, 4 * s + 1)
                eng.tensor_tensor(hid_mean2[:, :], hid_mean[:, :], hid_mean[:, :], ALU.mult).then_inc(hid_stats, 1)
                eng.wait_ge(hid_stats, 4 * s + 2)
                eng.scalar_tensor_tensor(hid_var[:, :], ps[:, SQ_BANK, SQ_COL:SQ_COL + 2 * NT:2], 1.0 / HID, hid_mean2[:, :],
                                         ALU.mult, ALU.subtract).then_inc(hid_stats, 1)
                eng.wait_ge(hid_stats, 4 * s + 3)
                eng.tensor_scalar(hid_var_eps[:, :], hid_var[:, :], 0.0, LN_EPS, ALU.max, ALU.add).then_inc(hid_stats, 1)

            def hidden_out(s):
                eng.wait_ge(hid_rstd_ready, s + 1)
                for t in range(NT):
                    eng.scalar_tensor_tensor(mix[:, t, :], ps[:, 4 + t, 0:D], hid_rstd[:, t:t + 1], beta_row[:, :],
                                             ALU.mult, ALU.add).then_inc(y_ready, 1)
                for t in range(NT):
                    eng.wait_ge(y_hi_ready, 4 * s + t + 1)
                    low(node_lo[:, t, :], mix[:, t, :], node_hi[:, t, 0:D], y_lo_ready)

            def moments(n, stats, mean_sum, mean_gap, square_dev, gap_square, mean, factor, var_eps, stats_done, done):
                eng.wait_ge(stats_done, 4 * (n + 1))
                eng.tensor_tensor(mean_gap[:, :], stats[:, :, 1], stats[:, :, 4], ALU.subtract).then_inc(done, 1)
                eng.tensor_tensor(mean_sum[:, :], stats[:, :, 1], stats[:, :, 4], ALU.add).then_inc(done, 1)
                eng.scalar_tensor_tensor(square_dev[:, :], stats[:, :, 2], D * LN_EPS, stats[:, :, 5],
                                         ALU.add, ALU.add).then_inc(done, 1)
                eng.wait_ge(done, 6 * n + 1)
                eng.scalar_tensor_tensor(gap_square[:, :], mean_gap[:, :], 0.25, mean_gap[:, :],
                                         ALU.mult, ALU.mult).then_inc(done, 1)
                eng.wait_ge(done, 6 * n + 2)
                eng.tensor_scalar(mean[:, :], mean_sum[:, :], factor, None, ALU.mult).then_inc(done, 1)
                eng.wait_ge(done, 6 * n + 4)
                eng.scalar_tensor_tensor(var_eps[:, :], square_dev[:, :], 1.0 / D, gap_square[:, :],
                                         ALU.mult, ALU.add).then_inc(done, 1)

            def residual_sum(s):
                eng.wait_ge(resid_ready, 4 * (s + 1))
                for t in range(NT):
                    eng.wait_ge(scatter2_psum, 2 * s + t // 2 + 1)
                    eng.scalar_tensor_tensor(resid[:, t, :], half(4, t), Dn[:, t:t + 1], resid[:, t, :],
                                             ALU.mult, ALU.add).then_inc(sum_ready, 1)
                for t in range(NT):
                    eng.wait_ge(sum_ready, 4 * s + t + 1)
                    eng.bn_stats(stats0[:, t, :], resid[:, t, :]).then_inc(sum_stats, 1)
                moments(s, stats0, mean_sum0, mean_gap0, square_dev0, gap_square0, mean0, 0.5, var_eps0,
                        sum_stats, sum_moments)

            def normalise(s):
                eng.wait_ge(rstd0_ready, s + 1)
                wait(eng, X_copied, s)
                for t in range(NT):
                    eng.tensor_scalar(X[:, t, :], resid[:, t, :], mean0[:, t:t + 1], rstd0[:, t:t + 1],
                                      ALU.subtract, ALU.mult).then_inc(X_ready, 1)

            def XT_low(r):
                for d in range(DT):
                    eng.wait_ge(XT_hi_ready, 2 * r + d + 1)
                    low(XT_lo[:, d, :], ps[:, XT_BANKS[d], :], XT_hi[:, d, :], XT_lo_ready)

            def z2_low(r):
                eng.wait_ge(z2_psum, 4 * (r + 1))
                eng.tensor_copy(score_i[:, :], ps[:, 4:4 + NT, D + 2]).then_inc(score_i_ready, 1)
                wait(eng, exp_slope_ready, 4 * r)
                eng.tensor_scalar(bias_j[:, :], ps[:, 4:4 + NT, D], score_dots[:, 3:4], None,
                                  ALU.add).then_inc(bias_j_ready, 1)
                eng.tensor_scalar(bias_j_slope[:, :], ps[:, 4:4 + NT, D], score_dots[:, 3:4], SLOPE,
                                  ALU.add, ALU.mult).then_inc(bias_j_ready, 1)
                for t in range(NT):
                    eng.wait_ge(z2_hi_ready, 4 * r + t + 1)
                    low(z2_lo[:, t, :], ps[:, 4 + t, 0:D], z2_hi[:, t, 0:D], z2_lo_ready)

            def larger_exponential(r, j):
                eng.wait_ge(exp_ready, 4 * r + j + 1)
                eng.wait_ge(exp_slope_ready, 4 * r + j + 1)
                eng.tensor_tensor(expo[:, j, :], expo[:, j, :], expo_slope[:, j % 2, :],
                                  ALU.max).then_inc(exp_larger, 1)

            def attention_low(r, j):
                eng.wait_ge(att_hi_ready, 4 * r + j + 1)
                low(att_lo[:, j, :], expo[:, j, :], att_hi[:, j, :], att_lo_ready)

            def shift_z0(r, t):
                if not isinstance(r, int) or r > 0:
                    eng.wait_ge(out_ready, 4 * (r - 1) + t + 1)
                eng.wait_ge(z1_ready, 4 * r + t + 1)
                eng.tensor_tensor(z0[:, t, :], ps[:, Z10_BANKS[t], D:2 * D], bk_row[:, :], ALU.add).then_inc(z0_ready, 1)

            def first_hop(r):
                eng.wait_ge(hop1_psum, 4 * (r + 1))
                eng.tensor_scalar(row_sum[:, :], ps[:, 0:NT, D], ROW_EPS, None, ALU.add).then_inc(rows_summed, 1)
                eng.wait_ge(rows_summed, r + 1)
                eng.reciprocal(row_inv[:, :], row_sum[:, :]).then_inc(row_inv_ready, 1)
                eng.wait_ge(row_inv_ready, r + 1)
                for t in range(NT):
                    eng.scalar_tensor_tensor(z1[:, t, :], ps[:, t, 0:D], row_inv[:, t:t + 1], z1[:, t, :],
                                             ALU.mult, ALU.add).then_inc(hop_ready, 1)
                for t in range(NT):
                    eng.wait_ge(hop_hi_ready, 4 * r + t + 1)
                    low(turn_lo[:, t * D:(t + 1) * D], z1[:, t, :], turn_hi[:, t * D:(t + 1) * D], hop_lo_ready)

            def last_hop_sum(r):
                for t in range(NT):
                    eng.wait_ge(hop2_psum, 2 * r + t // 2 + 1)
                    eng.scalar_tensor_tensor(z0[:, t, :], half(6, t), row_inv[:, t:t + 1], z0[:, t, :],
                                             ALU.mult, ALU.add).then_inc(hop2_added, 1)

            def last_relu(r):
                eng.wait_ge(hop2_added, 4 * (r + 1))
                eng.wait_ge(X_copied, r + 1)
                eng.scalar_tensor_tensor(z0[:, :, :], z0[:, :, :], 0.0, X_kept,
                                         ALU.max, ALU.add).then_inc(relu_added, 1)

            def last_stats(r):
                eng.wait_ge(relu_added, r + 1)
                for t in range(NT):
                    eng.bn_stats(stats1[:, t, :], z0[:, t, :]).then_inc(out_stats, 1)

            def last_moments(r):
                moments(r, stats1, mean_sum1, mean_gap1, square_dev1, gap_square1, neg_mean1, -0.5, var_eps1,
                        out_stats, out_moments)

            def layer0():
                setup()
                split_input(0)
                transpose_incidence(0)
                edges(0)
                degrees(0)
                turn_low(0)
                split_hidden(0)
                split_squares(0)
                hidden_norm(0)
                hidden_out(0)
                edges2(0)
                split_input(1)
                residual_sum(0)
                transpose_incidence(1)

            def body(r, last_hop, first_layer, prepare):
                s = r + 1
                normalise(r)
                if first_layer:
                    edges(s)
                if last_hop:
                    last_hop_sum(r - 1)
                XT_low(r)
                if last_hop:
                    last_relu(r - 1)
                if first_layer:
                    degrees(s)
                if last_hop:
                    last_stats(r - 1)
                z2_low(r)
                if first_layer:
                    turn_low(s)
                larger_exponential(r, 0)
                if last_hop:
                    last_moments(r - 1)
                for j in range(1, NT):
                    larger_exponential(r, j)
                if first_layer:
                    split_hidden(s)
                attention_low(r, 0)
                attention_low(r, 1)
                attention_low(r, 2)
                attention_low(r, 3)
                if first_layer:
                    split_squares(s)
                for t in range(NT):
                    shift_z0(r, t)
                if first_layer:
                    hidden_norm(s)
                    hidden_out(s)
                first_hop(r)
                if first_layer:
                    edges2(s)
                if prepare:
                    split_input(s + 1)
                if first_layer:
                    residual_sum(s)
                if prepare:
                    transpose_incidence(s + 1)

            def finish(r):
                last_hop_sum(r)
                last_relu(r)
                last_stats(r)
                last_moments(r)

            samples(eng, layer0, body, finish)

        @block.tensor
        def _(eng):
            def setup():
                eng.wait_ge(weights_loaded, 16 * 5)
                eng.wait_ge(ident_ready, 2)
                for d in range(DT):
                    for t in range(HT):
                        last = eng.transpose(ps[:, d, t * P:(t + 1) * P], w1_raw[:, t, d * P:(d + 1) * P], ident[:, :])
                    last.then_inc(setup_pe, 1)
                for t in range(HT):
                    for d in range(DT):
                        last = eng.transpose(ps[:, 2 + t, d * P:(d + 1) * P], w2_raw[:, d, t * P:(t + 1) * P], ident[:, :])
                    last.then_inc(setup_pe, 1)
                eng.wait_ge(gp_consts, 2)
                eng.wait_ge(setup_dve, SETUP_GAMMA)
                eng.wait_ge(setup_act, DT + HT)
                for t in range(HT):
                    last = eng.matmul(ps[:, 6, 0:D], ones_wide, w2_gamma[:, t, :], start=(t == 0), stop=(t == HT - 1))
                last.then_inc(setup_pe, 1)
                for t in range(HT):
                    last = eng.matmul(ps[:, 7, 0:D], beta_wide[:, t, :], w2_plain[:, t, :], start=(t == 0), stop=(t == HT - 1))
                last.then_inc(setup_pe, 1)

            def product(dst, terms, done=None, waits=()):
                for n, (stationary, moving) in enumerate(terms):
                    for term, semaphore, count in waits:
                        if term == n:
                            eng.wait_ge(semaphore, count)
                    width = moving.shape[-1]
                    last = eng.matmul(dst[:, 0:width], stationary, moving, start=(n == 0), stop=(n == len(terms) - 1))
                if done is not None:
                    last.then_inc(done, 1)

            def tile(t):
                return slice(t * P, (t + 1) * P)

            def transpose_adj(s):
                eng.wait_ge(adj_loaded, 16 * (s + 1))
                for t in range(NT):
                    if t >= 2:
                        wait(eng, hop_ready, 4 * (s - 2) + t - 1)
                    for c in range(NT):
                        last = eng.transpose(ps[:, T_BANKS[t], tile(c)], adj_sb[:, c, tile(t)], ident[:, :])
                    last.then_inc(adjT_psum, 1)

            def gather1(s):
                eng.wait_ge(inc_ready, s + 1)
                eng.wait_ge(x_hi_ready, s + 1)
                eng.wait_ge(adjT_ready, 4 * (s + 1))
                wait(eng, hop_ready, 4 * (s - 1))
                for t in range(NT):
                    product(ps[:, t, :], [(inc[:, c, tile(t)], node_hi[:, c, :]) for c in range(NT)]
                            + [(inc[:, c, tile(t)], node_lo[:, c, :]) for c in range(NT)], gather1_psum,
                            [(NT, x_lo_ready, s + 1)] if t == 0 else ())

            def scatter1(s):
                eng.wait_ge(incT_ready, s + 1)
                eng.wait_ge(w_ready, s + 1)
                eng.wait_ge(edge_lo_ready, 8 * s + 1)
                for t in range(NT):
                    product(ps[:, t, :], [(incT[:, e, tile(t)], edge_hi[:, e, :]) for e in range(NT)]
                            + [(incT[:, e, tile(t)], edge_lo[:, e, :]) for e in range(NT)], scatter1_psum,
                            [(e, edge_hi_ready, 8 * s + e + 1) for e in range(1, NT)]
                            + [(NT + e, edge_lo_ready, 8 * s + e + 1) for e in range(1, NT)] if t == 0 else ())

            def turn(s):
                for t in range(NT):
                    eng.wait_ge(mix_scaled, 4 * s + max(t + 1, DT))
                    for d in range(DT):
                        last = eng.transpose(ps[:, TURN_BANKS[d], tile(t)], mix[:, t, tile(d)], ident[:, :])
                        if t == NT - 1:
                            last.then_inc(turn_psum, 1)

            def hidden(s):
                wait(eng, z2_lo_ready, 4 * s)
                hi = [turn_hi[:, d * C:(d + 1) * C] for d in range(DT)]
                lo = [turn_lo[:, d * C:(d + 1) * C] for d in range(DT)]
                for t in range(HT):
                    product(ps[:, W1_BANKS[t], :], [(w1_hi[:, d, tile(t)], hi[d]) for d in range(DT)]
                            + [(w1_lo[:, d, tile(t)], hi[d]) for d in range(DT)]
                            + [(w1_hi[:, d, tile(t)], lo[d]) for d in range(DT)], hid_psum,
                            [(d, turn_hi_ready, 2 * s + d + 1) for d in range(DT)]
                            + [(2 * DT + d, turn_lo_ready, 2 * s + d + 1) for d in range(DT)] if t == 0 else ())

            def hidden_product(s):
                for t in range(NT):
                    product(ps[:, 4 + t, :], [(hid_hi[:, h, tile(t)], w2_hi[:, h, :]) for h in range(HT)]
                            + [(hid_hi[:, h, tile(t)], w2_lo[:, h, :]) for h in range(HT)]
                            + [(hid_lo[:, h, tile(t)], w2_hi[:, h, :]) for h in range(HT)], w2_psum,
                            [(h, hid_hi_ready, 4 * s + h + 1) for h in range(HT)]
                            + [(2 * HT + h, hid_lo_ready, 4 * s + h + 1) for h in range(HT)] if t == 0 else ())

            def sum_squares(s):
                eng.wait_ge(square_lo_ready, s + 1)
                for t in range(NT):
                    product(ps[:, SQ_BANK, SQ_COL + 2 * t:SQ_COL + 2 * t + 2], 
                            [(square_hi[:, tile(t)], ones2[:, :]), (square_lo[:, tile(t)], ones2[:, :])],
                            square_psum if t == NT - 1 else None)

            def gather2(s):
                for t in range(NT):
                    product(half(4, t), [(inc[:, c, tile(t)], node_hi[:, c, 0:D]) for c in range(NT)]
                            + [(inc[:, c, tile(t)], node_lo[:, c, :]) for c in range(NT)],
                            gather2_psum if t % 2 else None,
                            [(c, y_hi_ready, 4 * s + c + 1) for c in range(NT)]
                            + [(NT + c, y_lo_ready, 4 * s + c + 1) for c in range(NT)] if t == 0 else ())

            def scatter2(s):
                eng.wait_ge(edge_lo_ready, 8 * s + 6)
                for t in range(NT):
                    product(half(4, t), [(incT[:, e, tile(t)], edge_hi[:, e, 0:D]) for e in range(NT)]
                            + [(incT[:, e, tile(t)], edge_lo[:, e, :]) for e in range(NT)],
                            scatter2_psum if t % 2 else None,
                            [(e, edge_hi_ready, 8 * s + 4 + e + 1) for e in range(2, NT)]
                            + [(NT + e, edge_lo_ready, 8 * s + 4 + e + 1) for e in range(2, NT)] if t == 0 else ())

            def transpose_X(r):
                eng.wait_ge(X_ready, 4 * (r + 1))
                for d in range(DT):
                    for t in range(NT):
                        last = eng.transpose(ps[:, XT_BANKS[d], tile(t)], X[:, t, tile(d)], ident[:, :])
                    last.then_inc(XT_psum, 1)

            def z2_product(r):
                eng.wait_ge(XT_lo_ready, 2 * r + 1)
                wait(eng, hop2_added, 4 * r)
                for t in range(NT):
                    product(ps[:, 4 + t, :], [(XT_hi[:, d, tile(t)], wk2_hi[:, d, :]) for d in range(DT)]
                            + [(XT_hi[:, d, tile(t)], wk2_lo[:, d, :]) for d in range(DT)]
                            + [(XT_lo[:, d, tile(t)], wk2_hi[:, d, :]) for d in range(DT)], z2_psum,
                            [(1, XT_hi_ready, 2 * r + 2), (2 * DT + 1, XT_lo_ready, 2 * r + 2)] if t == 0 else ())

            def spread_scores(r, first_layer):
                if first_layer:
                    eng.wait_ge(mix_scaled, 4 * (r + 2))
                else:
                    eng.wait_ge(hop_ready, 4 * r)
                eng.wait_ge(score_i_ready, r + 1)
                for t in range(NT):
                    last = eng.transpose(ps[:, SI_BANK, tile(t)], score_i[:, t:t + 1].to_broadcast([P, P]), ident[:, :])
                last.then_inc(si_psum, 1)

            def z10_product(r, t):
                if Z10_BANKS[t] == SI_BANK:
                    eng.wait_ge(exp_slope_ready, 4 * (r + 1))
                product(ps[:, Z10_BANKS[t], :], [(XT_hi[:, d, tile(t)], wk10_hi[:, d, :]) for d in range(DT)]
                        + [(XT_lo[:, d, tile(t)], wk10_hi[:, d, :]) for d in range(DT)]
                        + [(XT_hi[:, d, tile(t)], wk10_lo[:, d, :]) for d in range(DT)], z10_psum)

            def first_hop(r):
                eng.wait_ge(z2_lo_ready, 4 * (r + 1))
                eng.wait_ge(z0_ready, 4 * (r + 1))
                for t in range(NT):
                    product(ps[:, t, :], [(att_hi[:, j, tile(t)], z2_hi[:, j, :]) for j in range(NT)]
                            + [(att_hi[:, j, tile(t)], z2_lo[:, j, :]) for j in range(NT)]
                            + [(att_lo[:, j, tile(t)], z2_hi[:, j, :]) for j in range(NT)], hop1_psum,
                            [(j, att_hi_ready, 4 * r + j + 1) for j in range(NT)]
                            + [(2 * NT + j, att_lo_ready, 4 * r + j + 1) for j in range(NT)] if t == 0 else ())

            def last_hop_product(r):
                eng.wait_ge(adjT_ready, min(4 * (r + 3), 4 * B) if isinstance(r, int) else 4 * (r + 3))
                hi = [turn_hi[:, j * D:(j + 1) * D] for j in range(NT)]
                lo = [turn_lo[:, j * D:(j + 1) * D] for j in range(NT)]
                for t in range(NT):
                    product(half(6, t), [(att_hi[:, j, tile(t)], hi[j]) for j in range(NT)]
                            + [(att_lo[:, j, tile(t)], hi[j]) for j in range(NT)]
                            + [(att_hi[:, j, tile(t)], lo[j]) for j in range(NT)],
                            hop2_psum if t % 2 else None,
                            [(j, hop_hi_ready, 4 * r + j + 1) for j in range(NT)]
                            + [(2 * NT + j, hop_lo_ready, 4 * r + j + 1) for j in range(NT)] if t == 0 else ())

            def layer0():
                setup()
                eng.wait_ge(setup_dve, SETUP_DONE)
                transpose_adj(0)
                gather1(0)
                scatter1(0)
                turn(0)
                hidden(0)
                hidden_product(0)
                sum_squares(0)
                gather2(0)
                transpose_adj(1)
                scatter2(0)

            def body(r, last_hop, first_layer, prepare):
                s = r + 1
                if first_layer:
                    gather1(s)
                if last_hop:
                    last_hop_product(r - 1)
                transpose_X(r)
                if first_layer:
                    scatter1(s)
                z2_product(r)
                if first_layer:
                    turn(s)
                spread_scores(r, first_layer)
                z10_product(r, 0)
                if first_layer:
                    hidden(s)
                for t in range(1, NT):
                    z10_product(r, t)
                if first_layer:
                    hidden_product(s)
                    sum_squares(s)
                first_hop(r)
                if first_layer:
                    gather2(s)
                if prepare:
                    transpose_adj(s + 1)
                if first_layer:
                    scatter2(s)

            samples(eng, layer0, body, last_hop_product)


_INS = ['x', 'adj', 'L0_gnn_W1', 'L0_gnn_b1', 'L0_gnn_gamma', 'L0_gnn_beta', 'L0_gnn_W2', 'L0_gnn_b2',
        'L1_gnn_Wv', 'L1_gnn_bv', 'L1_gnn_aw', 'L1_gnn_ab', 'L1_gnn_Wk', 'L1_gnn_bk']
_OUTS = [((16, 512, 256), 'float32')]


def kernel(**inputs):
    import numpy as _np
    import concourse.bacc as _bacc
    from concourse import mybir as _mybir
    from concourse.bass_utils import run_bass_kernel_spmd as _run

    nc = _bacc.Bacc("TRN2", target_bir_lowering=False, num_devices=1)
    arrays, args = {}, []
    for name in _INS:
        a = _np.ascontiguousarray(inputs[name])
        arrays[f"in_{name}_dram"] = a
        args.append(nc.dram_tensor(f"in_{name}_dram", a.shape, _mybir.dt.from_np(a.dtype), kind="ExternalInput").ap())
    for i, (shape, dtype) in enumerate(_OUTS):
        dt = _mybir.dt.from_np(_np.dtype(dtype))
        args.append(nc.dram_tensor(f"out_{i}_dram", shape, dt, kind="ExternalOutput").ap())
    resnorm_hypergraph_attention_kernel(nc, *args)
    r = _run(nc, [arrays], core_ids=[0])
    got = tuple(r.results[0][f"out_{i}_dram"] for i in range(len(_OUTS)))
    return got[0]
```

```python
import numpy as np
import concourse.bass as bass
from concourse import mybir
from contextlib import ExitStack


def resnorm_hypergraph_attention_kernel(
    nc: bass.Bass,
    x: bass.AP,
    adj: bass.AP,
    W1: bass.AP,
    b1: bass.AP,
    gamma: bass.AP,
    beta: bass.AP,
    W2: bass.AP,
    b2: bass.AP,
    Wv: bass.AP,
    bv: bass.AP,
    aw: bass.AP,
    ab: bass.AP,
    Wk: bass.AP,
    bk: bass.AP,
    out: bass.AP,
):
    f32 = mybir.dt.float32
    f32r = mybir.dt.float32r
    ALU = mybir.AluOpType
    ACT = mybir.ActivationFunctionType
    AX = mybir.AxisListType

    P = 128
    B, C, D = x.shape
    HID = W1.shape[0]
    K = Wk.shape[0]
    NT, DT, HT = C // P, D // P, HID // P
    DE = D + 2
    LN_EPS = 1e-5
    ROW_EPS = 1e-12
    SLOPE = 0.2
    SMALLEST = float(np.finfo(np.float32).tiny)
    assert K == 3 and NT == 4 and DT == 2 and HT == 4

    ctx = ExitStack()
    with ctx:
        def sb(name, shape, dt=f32):
            return ctx.enter_context(nc.sbuf_tensor(name, shape, dt))

        def sem(name):
            return ctx.enter_context(nc.semaphore(name))

        ident = sb("ident", [P, P])
        ones_col = sb("ones_col", [P, 1])
        minus_half = sb("minus_half", [P, NT])
        w1_hi = sb("w1_hi", [P, DT, HID], f32r)
        w1_lo = sb("w1_lo", [P, DT, HID], f32r)
        w2_hi = sb("w2_hi", [P, HT, DE], f32r)
        w2_lo = sb("w2_lo", [P, HT, D], f32r)
        wk2_hi = sb("wk2_hi", [P, DT, D + 4], f32r)
        wk2_lo = sb("wk2_lo", [P, DT, D + 4], f32r)
        wk10_hi = sb("wk10_hi", [P, DT, 2 * D], f32r)
        wk10_lo = sb("wk10_lo", [P, DT, 2 * D], f32r)
        b1_col = sb("b1_col", [P, HT])
        gamma_col = sb("gamma_col", [P, HT])
        beta_col = sb("beta_col", [P, HT])
        beta_row = sb("beta_row", [P, D])
        b2_row = sb("b2_row", [P, D])
        bk_row = sb("bk_row", [P, D])
        score_dots = sb("score_dots", [P, 4])
        wv_dots = sb("wv_dots", [P, DT, 2])

        adj_sb = sb("adj_sb", [P, NT, C])
        inc = sb("inc", [P, NT, C], f32r)
        incT = sb("incT", [P, NT, C], f32r)
        adjT = sb("adjT", [P, 2, NT, C])
        x_sb = sb("x_sb", [P, NT, D])
        node_hi = sb("node_hi", [P, NT, DE], f32r)
        node_lo = sb("node_lo", [P, NT, D], f32r)
        edge_hi = sb("edge_hi", [P, NT, DE], f32r)
        edge_lo = sb("edge_lo", [P, NT, D], f32r)
        resid = sb("resid", [P, NT, D])
        mix = sb("mix", [P, NT, D])
        turn_hi = sb("turn_hi", [P, DT * C], f32r)
        turn_lo = sb("turn_lo", [P, DT * C], f32r)
        hid = sb("hid", [P, HT, C])
        hid_hi = sb("hid_hi", [P, HT, C], f32r)
        hid_lo = sb("hid_lo", [P, HT, C], f32r)
        square = sb("square", [P, 2, C])
        square_sum = sb("square_sum", [P, C])

        X_pair = sb("X_pair", [P, 2, NT, D])
        X = X_pair[:, 0, :, :]
        X_kept = X_pair[:, 1, :, :]
        XT_hi = sb("XT_hi", [P, DT, C], f32r)
        XT_lo = sb("XT_lo", [P, DT, C], f32r)
        expo = sb("expo", [P, NT, C])
        expo_slope = sb("expo_slope", [P, 2, C])
        att_hi = sb("att_hi", [P, NT, C], f32r)
        att_lo = sb("att_lo", [P, NT, C], f32r)
        z2_hi = sb("z2_hi", [P, NT, DE], f32r)
        z2_lo = sb("z2_lo", [P, NT, D], f32r)
        z1 = sb("z1", [P, NT, D])
        z0 = sb("z0", [P, NT, D])
        out_sb = sb("out_sb", [P, NT, D])

        nodes_of = sb("nodes_of", [P, NT])
        Be = sb("Be", [P, NT])
        D_sum = sb("D_sum", [P, NT])
        D_safe = sb("D_safe", [P, NT])
        D_inv = sb("D_inv", [P, NT])
        Dn = sb("Dn", [P, NT])
        hid_mean = sb("hid_mean", [P, NT])
        hid_mean2 = sb("hid_mean2", [P, NT])
        hid_var = sb("hid_var", [P, NT])
        hid_var_eps = sb("hid_var_eps", [P, NT])
        hid_rstd = sb("hid_rstd", [P, NT])
        stats0 = sb("stats0", [P, NT, 6])
        mean_sum0 = sb("mean_sum0", [P, NT])
        mean_gap0 = sb("mean_gap0", [P, NT])
        square_dev0 = sb("square_dev0", [P, NT])
        gap_square0 = sb("gap_square0", [P, NT])
        mean0 = sb("mean0", [P, NT])
        var_eps0 = sb("var_eps0", [P, NT])
        rstd0 = sb("rstd0", [P, NT])
        score_i = sb("score_i", [P, NT])
        bias_j = sb("bias_j", [P, NT])
        bias_j_slope = sb("bias_j_slope", [P, NT])
        row_sum = sb("row_sum", [P, NT])
        row_inv = sb("row_inv", [P, NT])
        stats1 = sb("stats1", [P, NT, 6])
        mean_sum1 = sb("mean_sum1", [P, NT])
        mean_gap1 = sb("mean_gap1", [P, NT])
        square_dev1 = sb("square_dev1", [P, NT])
        gap_square1 = sb("gap_square1", [P, NT])
        shift1 = sb("shift1", [P, NT])
        neg_mean1 = sb("neg_mean1", [P, NT])
        var_eps1 = sb("var_eps1", [P, NT])
        rstd1 = sb("rstd1", [P, NT])

        w1_raw = adjT[:, 1, 0:2, :].rearrange("p a n -> p (a n)").rearrange("p (t d) -> p t d", d=D)
        w2_raw = adjT[:, 1, 2:4, :]
        wk_raw = X_pair[:, :, :, :].rearrange("p a t d -> p (a t) d")
        beta_wide = X_pair[:, 1, 2:4, :].rearrange("p a d -> p (a d)").rearrange("p (t n) -> p t n", n=P)
        w2_gamma = out_sb[:, :, :]
        w2_plain = expo_slope[:, :, :].rearrange("p a n -> p (a n)").rearrange("p (t d) -> p t d", d=D)
        wv_raw = z1[:, 0:DT, :]
        bk_raw = z1[:, 2:4, :]
        aw_row = z0[:, 0:2, :]
        bv_row = z0[:, 2, :]
        dot_tmp = z0[:, 3, :]
        bk_raw2 = expo[:, 0, 0:D]
        wv_tmp = expo[:, 1, 0:D]
        ones_wide = expo[:, 2, 0:P]

        ps = ctx.enter_context(nc.psum_tensor("ps", [P, 8, 512], f32))
        T_BANKS = [6, 7, 0, 1]
        T1_BANKS = [0, 1, 2, 3]
        XT_BANKS = [4, 5]
        TURN_BANKS = [0, 1]
        W1T_BANKS = [4, 5]
        W2T_BANK = 6
        SUM_BANKS = [4, 5]
        W1_BANKS = [4, 5, 6, 7]
        SI_BANK = 3
        SQ_BANK, SQ_COL = 7, D + 8
        Z10_BANKS = [2, 0, 1, 3]
        Z10_LAST_BANKS = [2, 0, 1, 4]

        def z10_banks(r):
            return Z10_LAST_BANKS if isinstance(r, int) and r == B - 1 else Z10_BANKS

        def z0_of(r):
            return resid if isinstance(r, int) and r == B - 1 else z0

        def half(bank0, t):
            return ps[:, bank0 + t // 2, (t % 2) * D:(t % 2 + 1) * D]

        adj_loaded = sem("adj_loaded")
        x_loaded = sem("x_loaded")
        out_stored = sem("out_stored")
        w1_loaded = sem("w1_loaded")
        w2_loaded = sem("w2_loaded")
        wk_loaded = sem("wk_loaded")
        b2_loaded = sem("b2_loaded")
        cols_loaded = sem("cols_loaded")
        rows_loaded = sem("rows_loaded")
        ident_ready = sem("ident_ready")
        ones_wide_ready = sem("ones_wide_ready")
        powers_ready = sem("powers_ready")
        ones_ready = sem("ones_ready")
        beta_wide_ready = sem("beta_wide_ready")
        w1T_psum = sem("w1T_psum")
        w1_hi_ready = sem("w1_hi_ready")
        w1_lo_ready = sem("w1_lo_ready")
        w2T_psum = sem("w2T_psum")
        w2_plain_ready = sem("w2_plain_ready")
        w2_scaled = sem("w2_scaled")
        w2_sums_psum = sem("w2_sums_psum")
        w2_centred = sem("w2_centred")
        w2_split = sem("w2_split")
        wk_hi_ready = sem("wk_hi_ready")
        wk_lo_ready = sem("wk_lo_ready")
        dot_steps = sem("dot_steps")
        adjT_psum = sem("adjT_psum")
        gather1_psum = sem("gather1_psum")
        scatter1_psum = sem("scatter1_psum")
        turn_psum = sem("turn_psum")
        hid_psum = sem("hid_psum")
        w2_psum = sem("w2_psum")
        square_psum = sem("square_psum")
        gather2_psum = sem("gather2_psum")
        scatter2_psum = sem("scatter2_psum")
        XT_psum = sem("XT_psum")
        z2_psum = sem("z2_psum")
        si_psum = sem("si_psum")
        z10_psum = sem("z10_psum")
        hop1_psum = sem("hop1_psum")
        hop2_psum = sem("hop2_psum")
        inc_ready = sem("inc_ready")
        incT_ready = sem("incT_ready")
        adjT_ready = sem("adjT_ready")
        w_hi_ready = sem("w_hi_ready")
        w_ready = sem("w_ready")
        x_hi_ready = sem("x_hi_ready")
        x_lo_ready = sem("x_lo_ready")
        twice_x = sem("twice_x")
        resid_ready = sem("resid_ready")
        nodes_counted = sem("nodes_counted")
        Be_ready = sem("Be_ready")
        edge_hi_ready = sem("edge_hi_ready")
        edge_lo_ready = sem("edge_lo_ready")
        D_summed = sem("D_summed")
        D_clamped = sem("D_clamped")
        D_inverted = sem("D_inverted")
        Dn_ready = sem("Dn_ready")
        mix_scaled = sem("mix_scaled")
        turn_hi_ready = sem("turn_hi_ready")
        turn_lo_ready = sem("turn_lo_ready")
        hid_ready = sem("hid_ready")
        hid_hi_ready = sem("hid_hi_ready")
        hid_lo_ready = sem("hid_lo_ready")
        squared = sem("squared")
        squares_added = sem("squares_added")
        hid_stats = sem("hid_stats")
        hid_rstd_ready = sem("hid_rstd_ready")
        y_ready = sem("y_ready")
        y_hi_ready = sem("y_hi_ready")
        y_lo_ready = sem("y_lo_ready")
        sum_ready = sem("sum_ready")
        sum_stats = sem("sum_stats")
        sum_moments = sem("sum_moments")
        rstd0_ready = sem("rstd0_ready")
        X_ready = sem("X_ready")
        X_copied = sem("X_copied")
        XT_hi_ready = sem("XT_hi_ready")
        XT_lo_ready = sem("XT_lo_ready")
        bias_j_ready = sem("bias_j_ready")
        score_i_ready = sem("score_i_ready")
        z2_hi_ready = sem("z2_hi_ready")
        z2_lo_ready = sem("z2_lo_ready")
        exp_ready = sem("exp_ready")
        exp_slope_ready = sem("exp_slope_ready")
        exp_larger = sem("exp_larger")
        att_ready = sem("att_ready")
        att_hi_ready = sem("att_hi_ready")
        att_lo_ready = sem("att_lo_ready")
        z1_ready = sem("z1_ready")
        z0_ready = sem("z0_ready")
        rows_summed = sem("rows_summed")
        row_inv_ready = sem("row_inv_ready")
        hop_ready = sem("hop_ready")
        hop_hi_ready = sem("hop_hi_ready")
        hop_lo_ready = sem("hop_lo_ready")
        hop2_added = sem("hop2_added")
        relu_added = sem("relu_added")
        out_stats = sem("out_stats")
        out_moments = sem("out_moments")
        rstd1_ready = sem("rstd1_ready")
        shift1_ready = sem("shift1_ready")
        out_ready = sem("out_ready")

        def wait(eng, semaphore, count):
            if not isinstance(count, int) or count > 0:
                eng.wait_ge(semaphore, count)

        def samples(eng, layer0, body, finish):
            layer0()
            body(0, False, True, True)
            body(1, True, True, True)
            with eng.Fori(2, B - 2) as r:
                body(r, True, True, True)
            body(B - 2, True, True, False)
            body(B - 1, True, False, False)
            finish(B - 1)

        DOT_STEPS = 2 + 4 + 1 + 8 + 4

        hops = ((2, wk2_hi, wk2_lo, 0), (1, wk10_hi, wk10_lo, 0), (0, wk10_hi, wk10_lo, D))

        block = ctx.enter_context(nc.Block())

        @block.sync
        def _(eng):
            def load_adj(s):
                wait(eng, inc_ready, s)
                wait(eng, adjT_psum, 4 * s)
                eng.dma_start(adj_sb[:, :, :], adj[s].rearrange("(t p) e -> p t e", p=P)).then_inc(adj_loaded, 16)

            def load_x(s):
                wait(eng, x_lo_ready, s)
                wait(eng, twice_x, s)
                eng.dma_start(x_sb[:, :, :], x[s].rearrange("(t p) d -> p t d", p=P)).then_inc(x_loaded, 16)

            def store_out(r):
                eng.wait_ge(out_ready, 4 * (r + 1))
                eng.dma_start(out[r].rearrange("(t p) d -> p t d", p=P), out_sb[:, :, :]).then_inc(out_stored, 16)

            def layer0():
                load_adj(0)
                load_x(0)
                for col, v in ((gamma_col, gamma), (beta_col, beta), (b1_col, b1)):
                    eng.dma_start(col[:, :], v.rearrange("(t p) -> p t", p=P),
                                  allow_slow_non_contiguous=True).then_inc(cols_loaded, 16)
                eng.dma_start(b2_row[:, :], b2.rearrange("(a n) -> a n", a=1).to_broadcast([P, D])).then_inc(b2_loaded, 16)
                eng.dma_start(aw_row, aw.rearrange("(a n) b -> b a n", a=2).to_broadcast([P, 2, D])).then_inc(rows_loaded, 16)
                eng.dma_start(bv_row, bv.rearrange("(a n) -> a n", a=1).to_broadcast([P, D])).then_inc(rows_loaded, 16)
                eng.dma_start(score_dots[:, 2:3], ab.rearrange("(a n) -> a n", a=1).to_broadcast([P, 1])).then_inc(rows_loaded, 16)
                eng.dma_start(bk_raw[:, 0, :], bk[0:1, :].to_broadcast([P, D])).then_inc(rows_loaded, 16)
                eng.dma_start(bk_raw[:, 1, :], bk[1:2, :].to_broadcast([P, D])).then_inc(rows_loaded, 16)
                eng.dma_start(bk_raw2, bk[2:3, :].to_broadcast([P, D])).then_inc(rows_loaded, 16)
                load_adj(1)

            def addresses(r):
                if not isinstance(r, int):
                    eng.compute_val(4 * (r + 2))
                    eng.compute_val((r + 1) * (C * D) * 4)
                    eng.compute_val((r + 2) * (C * C) * 4)
                    eng.compute_val((r - 1) * (C * D) * 4)

            def body(r, last_hop, first_layer, prepare):
                addresses(r)
                if first_layer:
                    load_x(r + 1)
                if prepare:
                    load_adj(r + 2)
                if last_hop:
                    store_out(r - 1)

            def finish(r):
                store_out(r)

            samples(eng, layer0, body, finish)
            eng.wait_ge(out_stored, 16 * B)

        @block.gpsimd
        def _(eng):
            eng.memset(ident[:, :], 0.0).then_inc(ident_ready, 1)
            eng.wait_ge(ident_ready, 1)
            eng.affine_select(out=ident[:, :], in_=ident[:, :], compare_op=ALU.not_equal, fill=1.0,
                              base=0, pattern=[[-1, P]], channel_multiplier=1).then_inc(ident_ready, 1)
            eng.memset(ones_wide, 1.0).then_inc(ones_wide_ready, 1)
            eng.memset(minus_half[:, :], -0.5).then_inc(powers_ready, 1)

            def double_x(s):
                eng.wait_ge(x_loaded, 16 * (s + 1))
                wait(eng, X_ready, 4 * s)
                eng.tensor_tensor(resid[:, :, :], x_sb[:, :, :], x_sb[:, :, :], ALU.add).then_inc(twice_x, 1)
                eng.wait_ge(twice_x, s + 1)
                for t in range(NT):
                    eng.tensor_tensor(resid[:, t, :], resid[:, t, :], b2_row[:, :], ALU.add).then_inc(resid_ready, 1)

            def power_out(r):
                eng.wait_ge(out_moments, 6 * (r + 1))
                wait(eng, out_ready, 4 * r)
                eng.tensor_tensor(rstd1[:, :], var_eps1[:, :], minus_half[:, :], ALU.pow).then_inc(rstd1_ready, 1)
                eng.wait_ge(rstd1_ready, r + 1)
                eng.tensor_tensor(shift1[:, :], neg_mean1[:, :], rstd1[:, :], ALU.mult).then_inc(shift1_ready, 1)

            def weigh_attention(r):
                eng.wait_ge(adjT_ready, 4 * (r + 1))
                for j in range(NT):
                    eng.wait_ge(exp_larger, 4 * r + j + 1)
                    eng.tensor_tensor(expo[:, j, :], expo[:, j, :], adjT[:, r % 2, j, :],
                                      ALU.mult).then_inc(att_ready, 1)

            def add_squares(s):
                eng.wait_ge(squared, 4 * s + 2)
                wait(eng, square_psum, s)
                eng.tensor_tensor(square_sum[:, :], square[:, 0, :], square[:, 1, :], ALU.add).then_inc(squares_added, 1)
                for t in range(2, HT):
                    eng.wait_ge(squared, 4 * s + t + 1)
                    eng.wait_ge(squares_added, 3 * s + t - 1)
                    eng.tensor_tensor(square_sum[:, :], square_sum[:, :], square[:, t % 2, :],
                                      ALU.add).then_inc(squares_added, 1)

            def power_hidden(s):
                eng.wait_ge(hid_stats, 4 * (s + 1))
                eng.tensor_tensor(hid_rstd[:, :], hid_var_eps[:, :], minus_half[:, :], ALU.pow).then_inc(hid_rstd_ready, 1)

            def power_sum(s):
                eng.wait_ge(sum_moments, 6 * (s + 1))
                eng.tensor_tensor(rstd0[:, :], var_eps0[:, :], minus_half[:, :], ALU.pow).then_inc(rstd0_ready, 1)

            def layer0():
                eng.wait_ge(powers_ready, 1)
                eng.wait_ge(b2_loaded, 16)
                double_x(0)
                for n, (k, hi, lo, c0) in enumerate(hops):
                    eng.wait_ge(wk_hi_ready, n + 1)
                    eng.tensor_tensor(lo[:, :, c0:c0 + D], wk_raw[:, k * DT:(k + 1) * DT, :],
                                      hi[:, :, c0:c0 + D].bitcast(f32), ALU.subtract).then_inc(wk_lo_ready, 1)
                add_squares(0)
                power_hidden(0)
                power_sum(0)

            def body(r, last_hop, first_layer, prepare):
                s = r + 1
                if first_layer:
                    double_x(s)
                weigh_attention(r)
                if last_hop:
                    power_out(r - 1)
                if first_layer:
                    add_squares(s)
                if first_layer:
                    power_hidden(s)
                    power_sum(s)

            samples(eng, layer0, body, power_out)

        @block.scalar
        def _(eng):
            eng.dma_start(w1_raw, W1.rearrange("(t p) d -> p t d", p=P)).then_inc(w1_loaded, 16)
            eng.dma_start(w2_raw, W2.rearrange("(t p) h -> p t h", p=P)).then_inc(w2_loaded, 16)
            eng.dma_start(wk_raw[:, 0:K * DT, :], Wk.rearrange("k (t p) o -> p (k t) o", p=P)).then_inc(wk_loaded, 16)
            eng.dma_start(wv_raw, Wv.rearrange("(t p) o -> p t o", p=P)).then_inc(rows_loaded, 16)

            def split_w1():
                for d in range(DT):
                    eng.wait_ge(w1T_psum, d + 1)
                    eng.activation(w1_hi[:, d, :], ps[:, W1T_BANKS[d], :], ACT.Copy).then_inc(w1_hi_ready, 1)

            def copy_w2():
                for t in range(HT):
                    eng.wait_ge(w2T_psum, 2 * (t // 2) + 2)
                    eng.activation(w2_plain[:, t, :], half(W2T_BANK, t), ACT.Copy).then_inc(w2_plain_ready, 1)

            def split_wk():
                eng.wait_ge(wk_loaded, 16)
                for k, hi, lo, c0 in hops:
                    eng.activation(hi[:, :, c0:c0 + D], wk_raw[:, k * DT:(k + 1) * DT, :],
                                   ACT.Copy).then_inc(wk_hi_ready, 1)

            def split_edges(s, conv):
                eng.wait_ge(Be_ready, s + 1)
                wait(eng, scatter2_psum if conv == 0 else scatter1_psum, 2 * s if conv == 0 else 4 * (s + 1))
                for t in range(NT):
                    if conv == 0:
                        src = ps[:, t, 0:D]
                    else:
                        eng.wait_ge(gather2_psum, 2 * s + t // 2 + 1)
                        src = half(4, t)
                    eng.activation(edge_hi[:, t, 0:D], src, ACT.Copy, scale=Be[:, t:t + 1]).then_inc(edge_hi_ready, 1)

            def split_XT(r):
                wait(eng, z10_psum, 4 * r)
                for d in range(DT):
                    eng.wait_ge(XT_psum, 2 * r + d + 1)
                    eng.activation(XT_hi[:, d, :], ps[:, XT_BANKS[d], :], ACT.Copy).then_inc(XT_hi_ready, 1)

            def keep_X(r):
                eng.wait_ge(X_ready, 4 * (r + 1))
                wait(eng, relu_added, r)
                eng.activation(X_kept, X, ACT.Copy).then_inc(X_copied, 1)

            def normalise_out(r, tiles=range(NT)):
                eng.wait_ge(shift1_ready, r + 1)
                wait(eng, out_stored, 16 * r)
                for t in tiles:
                    eng.activation(out_sb[:, t, :], z0_of(r)[:, t, :], ACT.Identity, bias=shift1[:, t:t + 1],
                                   scale=rstd1[:, t:t + 1]).then_inc(out_ready, 1)

            def scale_mix(s):
                eng.wait_ge(Dn_ready, s + 1)
                wait(eng, y_lo_ready, 4 * s)
                for t in range(NT):
                    eng.activation(mix[:, t, :], ps[:, t, 0:D], ACT.Copy, scale=Dn[:, t:t + 1]).then_inc(mix_scaled, 1)

            def split_z2(r):
                eng.wait_ge(bias_j_ready, 2 * (r + 1))
                wait(eng, hop1_psum, 4 * r)
                for t in range(NT):
                    eng.activation(z2_hi[:, t, 0:D], ps[:, 4 + t, 0:D], ACT.Copy).then_inc(z2_hi_ready, 1)

            def exponentials(r, j):
                if j == 0:
                    eng.wait_ge(si_psum, r + 1)
                if j < 2:
                    wait(eng, exp_larger, 4 * r)
                else:
                    eng.wait_ge(exp_larger, 4 * r + j - 1)
                if j == 0:
                    wait(eng, att_lo_ready, 4 * r)
                eng.activation(expo[:, j, :], ps[:, SI_BANK, :], ACT.Exp,
                               bias=bias_j[:, j:j + 1]).then_inc(exp_ready, 1)
                eng.activation(expo_slope[:, j % 2, :], ps[:, SI_BANK, :], ACT.Exp,
                               bias=bias_j_slope[:, j:j + 1], scale=SLOPE).then_inc(exp_slope_ready, 1)

            def split_attention(r, j):
                if j == 0:
                    wait(eng, hop2_psum, 2 * r)
                eng.wait_ge(att_ready, 4 * r + j + 1)
                eng.activation(att_hi[:, j, :], expo[:, j, :], ACT.Copy).then_inc(att_hi_ready, 1)

            def split_turn(s):
                wait(eng, hop2_psum, 2 * (s - 1))
                for d in range(DT):
                    eng.wait_ge(turn_psum, 2 * s + d + 1)
                    eng.activation(turn_hi[:, d * C:(d + 1) * C], ps[:, TURN_BANKS[d], :],
                                   ACT.Copy).then_inc(turn_hi_ready, 1)

            def copy_z1(r, t):
                eng.wait_ge(z10_psum, 4 * r + t + 1)
                if t == 0:
                    wait(eng, hop_lo_ready, 4 * r)
                eng.activation(z1[:, t, :], ps[:, z10_banks(r)[t], 0:D], ACT.Copy).then_inc(z1_ready, 1)

            def hidden(s):
                wait(eng, hid_lo_ready, 4 * s)
                for t in range(HT):
                    eng.wait_ge(hid_psum, 4 * s + t + 1)
                    eng.activation(hid[:, t, :], ps[:, W1_BANKS[t], :], ACT.Relu,
                                   bias=b1_col[:, t:t + 1]).then_inc(hid_ready, 1)

            def squares(s, tiles):
                for t in tiles:
                    eng.wait_ge(hid_ready, 4 * s + t + 1)
                    if t >= 2:
                        eng.wait_ge(squares_added, 3 * s + 1)
                    else:
                        wait(eng, squares_added, 3 * s)
                    eng.activation(square[:, t % 2, :], hid[:, t, :], ACT.Square).then_inc(squared, 1)

            def split_y(s):
                for t in range(NT):
                    eng.wait_ge(y_ready, 4 * s + t + 1)
                    eng.activation(node_hi[:, t, 0:D], mix[:, t, :], ACT.Copy).then_inc(y_hi_ready, 1)

            def split_hop(r):
                for t in range(NT):
                    eng.wait_ge(hop_ready, 4 * r + t + 1)
                    eng.activation(turn_hi[:, t * D:(t + 1) * D], z1[:, t, :], ACT.Copy).then_inc(hop_hi_ready, 1)

            def copy_adjT(s, banks=T_BANKS):
                wait(eng, att_ready, 4 * (s - 1))
                for t in range(NT):
                    eng.wait_ge(adjT_psum, 4 * s + t + 1)
                    eng.activation(adjT[:, s % 2, t, :], ps[:, banks[t], :], ACT.Copy).then_inc(adjT_ready, 1)

            def layer0():
                copy_adjT(0)
                split_w1()
                split_edges(0, 0)
                copy_w2()
                scale_mix(0)
                split_turn(0)
                split_wk()
                eng.wait_ge(cols_loaded, 16 * 3)
                hidden(0)
                squares(0, range(HT))
                copy_adjT(1, T1_BANKS)
                split_y(0)
                split_edges(0, 1)

            def body(r, last_hop, first_layer, prepare):
                s = r + 1
                if first_layer:
                    split_edges(s, 0)
                split_XT(r)
                if first_layer:
                    scale_mix(s)
                split_z2(r)
                if first_layer:
                    split_turn(s)
                for j in range(NT):
                    exponentials(r, j)
                if first_layer:
                    hidden(s)
                    squares(s, (0, 1))
                split_attention(r, 0)
                copy_z1(r, 0)
                split_attention(r, 1)
                copy_z1(r, 1)
                if first_layer:
                    squares(s, (2, 3))
                split_attention(r, 2)
                split_attention(r, 3)
                copy_z1(r, 2)
                if last_hop and first_layer:
                    normalise_out(r - 1)
                copy_z1(r, 3)
                keep_X(r)
                if first_layer:
                    split_y(s)
                split_hop(r)
                if last_hop and not first_layer:
                    normalise_out(r - 1)
                if first_layer:
                    split_edges(s, 1)
                if prepare:
                    copy_adjT(s + 1)

            def finish(r):
                normalise_out(r, (0, 1))

            samples(eng, layer0, body, finish)

        @block.vector
        def _(eng):
            def low(dst, src, high, done):
                eng.tensor_tensor(dst, src, high.bitcast(f32), ALU.subtract).then_inc(done, 1)

            eng.memset(ones_col[:, :], 1.0).then_inc(ones_ready, 1)
            eng.memset(node_hi[:, :, D:DE].bitcast(f32), 1.0).then_inc(ones_ready, 1)
            eng.memset(z2_hi[:, :, D:DE].bitcast(f32), 1.0).then_inc(ones_ready, 1)
            eng.memset(w2_hi[:, :, D:DE].bitcast(f32), 1.0).then_inc(ones_ready, 1)

            def widen_beta():
                eng.wait_ge(cols_loaded, 16 * 3)
                eng.tensor_copy(beta_wide, beta_col[:, :].unsqueeze(2).to_broadcast([P, HT, P])).then_inc(beta_wide_ready, 1)

            def w1_low():
                for d in range(DT):
                    eng.wait_ge(w1_hi_ready, d + 1)
                    low(w1_lo[:, d, :], ps[:, W1T_BANKS[d], :], w1_hi[:, d, :], w1_lo_ready)

            def scale_w2():
                eng.wait_ge(w2_plain_ready, HT)
                for t in range(HT):
                    eng.tensor_scalar(w2_gamma[:, t, :], half(W2T_BANK, t), gamma_col[:, t:t + 1], None,
                                      ALU.mult).then_inc(w2_scaled, 1)

            def centre_w2():
                eng.wait_ge(w2_sums_psum, 2)
                for t in range(HT):
                    eng.scalar_tensor_tensor(w2_gamma[:, t, :], ps[:, SUM_BANKS[0], 0:D], -1.0 / HID, w2_gamma[:, t, :],
                                             ALU.mult, ALU.add).then_inc(w2_centred, 1)
                eng.tensor_copy(beta_row[:, :], ps[:, SUM_BANKS[1], 0:D]).then_inc(w2_centred, 1)
                eng.wait_ge(w2_centred, HT + 1)

            def split_w2():
                eng.tensor_copy(w2_hi[:, :, 0:D], w2_gamma).then_inc(w2_split, 1)
                eng.wait_ge(w2_split, 1)
                low(w2_lo[:, :, :], w2_gamma, w2_hi[:, :, 0:D], w2_split)

            def constant_dots():
                eng.wait_ge(rows_loaded, 16 * 7)
                eng.tensor_tensor(bk_row[:, :], bk_raw[:, 0, :], bk_raw[:, 1, :], ALU.add).then_inc(dot_steps, 1)
                eng.wait_ge(dot_steps, 1)
                eng.tensor_tensor(bk_row[:, :], bk_row[:, :], bk_raw2, ALU.add).then_inc(dot_steps, 1)
                for a in range(2):
                    eng.tensor_tensor(dot_tmp, bv_row, aw_row[:, a, :], ALU.mult).then_inc(dot_steps, 1)
                    eng.wait_ge(dot_steps, 2 + 2 * a + 1)
                    eng.reduce_sum(score_dots[:, a:a + 1], dot_tmp, axis=AX.X).then_inc(dot_steps, 1)
                    eng.wait_ge(dot_steps, 2 + 2 * a + 2)
                eng.reduce_sum(score_dots[:, 3:4], score_dots[:, 0:3], axis=AX.X).then_inc(dot_steps, 1)

            def weight_dots(d):
                done = 2 + 4 + 1 + 4 * d
                for a in range(2):
                    eng.tensor_tensor(wv_tmp, wv_raw[:, d, :], aw_row[:, a, :], ALU.mult).then_inc(dot_steps, 1)
                    eng.wait_ge(dot_steps, done + 1)
                    eng.reduce_sum(wv_dots[:, d, a:a + 1], wv_tmp, axis=AX.X).then_inc(dot_steps, 1)
                    done += 2
                    eng.wait_ge(dot_steps, done)

            def split_dots():
                done = 2 + 4 + 1 + 4 * DT
                for a in range(2):
                    v = wv_dots[:, :, a:a + 1].to_broadcast([P, DT, 2])
                    c0 = D + 2 * a
                    eng.tensor_copy(wk2_hi[:, :, c0:c0 + 2], v).then_inc(dot_steps, 1)
                    eng.wait_ge(dot_steps, done + 1)
                    low(wk2_lo[:, :, c0:c0 + 2], v, wk2_hi[:, :, c0:c0 + 2], dot_steps)
                    done += 2
                assert done == DOT_STEPS

            def split_input(s):
                eng.wait_ge(adj_loaded, 16 * (s + 1))
                wait(eng, gather2_psum, 2 * s)
                eng.tensor_scalar(inc[:, :, :], adj_sb[:, :, :], 0.0, None, ALU.not_equal).then_inc(inc_ready, 1)
                eng.wait_ge(x_loaded, 16 * (s + 1))
                eng.tensor_copy(node_hi[:, :, 0:D], x_sb[:, :, :]).then_inc(x_hi_ready, 1)
                eng.wait_ge(x_hi_ready, s + 1)
                low(node_lo[:, :, :], x_sb[:, :, :], node_hi[:, :, 0:D], x_lo_ready)

            def transpose_incidence(s):
                eng.wait_ge(adjT_ready, 4 * (s + 1))
                wait(eng, scatter2_psum, 2 * s)
                wait(eng, scatter1_psum, 4 * s)
                eng.tensor_scalar(incT[:, :, :], adjT[:, s % 2, :, :], 0.0, None, ALU.not_equal).then_inc(incT_ready, 1)
                w_col = adjT[:, s % 2, :, 0:1]
                eng.tensor_copy(edge_hi[:, :, D:D + 1], w_col).then_inc(w_hi_ready, 1)
                eng.wait_ge(w_hi_ready, s + 1)
                low(edge_hi[:, :, D + 1:DE], w_col, edge_hi[:, :, D:D + 1], w_ready)

            def edges(s):
                eng.wait_ge(gather1_psum, 4 * (s + 1))
                eng.tensor_scalar(nodes_of[:, :], ps[:, 0:NT, D], 1.0, None, ALU.max).then_inc(nodes_counted, 1)
                eng.wait_ge(nodes_counted, s + 1)
                eng.reciprocal(Be[:, :], nodes_of[:, :]).then_inc(Be_ready, 1)
                for t in range(NT):
                    eng.wait_ge(edge_hi_ready, 8 * s + t + 1)
                    eng.scalar_tensor_tensor(edge_lo[:, t, :], ps[:, t, 0:D], Be[:, t:t + 1],
                                             edge_hi[:, t, 0:D].bitcast(f32), ALU.mult, ALU.subtract)\
                       .then_inc(edge_lo_ready, 1)

            def edges2(s):
                for t in range(NT):
                    eng.wait_ge(edge_hi_ready, 8 * s + 4 + 2 * (t // 2) + 2)
                    eng.scalar_tensor_tensor(edge_lo[:, t, :], half(4, t), Be[:, t:t + 1],
                                             edge_hi[:, t, 0:D].bitcast(f32), ALU.mult, ALU.subtract)\
                       .then_inc(edge_lo_ready, 1)

            def degrees(s):
                eng.wait_ge(scatter1_psum, 4 * (s + 1))
                eng.reduce_sum(D_sum[:, :], ps[:, 0:NT, D:DE], axis=AX.X).then_inc(D_summed, 1)
                eng.wait_ge(D_summed, s + 1)
                eng.tensor_scalar(D_safe[:, :], D_sum[:, :], SMALLEST, None, ALU.max).then_inc(D_clamped, 1)
                eng.wait_ge(D_clamped, s + 1)
                eng.reciprocal(D_inv[:, :], D_safe[:, :]).then_inc(D_inverted, 1)
                eng.wait_ge(D_inverted, s + 1)
                eng.scalar_tensor_tensor(Dn[:, :], D_sum[:, :], 0.0, D_inv[:, :], ALU.is_gt, ALU.mult)\
                   .then_inc(Dn_ready, 1)

            def turn_low(s):
                for d in range(DT):
                    eng.wait_ge(turn_hi_ready, 2 * s + d + 1)
                    low(turn_lo[:, d * C:(d + 1) * C], ps[:, TURN_BANKS[d], :], turn_hi[:, d * C:(d + 1) * C],
                        turn_lo_ready)

            def split_hidden(s):
                wait(eng, w2_psum, 4 * s)
                for t in range(HT):
                    eng.wait_ge(hid_ready, 4 * s + t + 1)
                    eng.tensor_copy(hid_hi[:, t, :], hid[:, t, :]).then_inc(hid_hi_ready, 1)
                    eng.wait_ge(hid_hi_ready, 4 * s + t + 1)
                    low(hid_lo[:, t, :], hid[:, t, :], hid_hi[:, t, :], hid_lo_ready)

            def hidden_norm(s):
                eng.wait_ge(square_psum, s + 1)
                eng.tensor_scalar(hid_mean[:, :], ps[:, 4:4 + NT, D], 1.0 / HID, None, ALU.mult).then_inc(hid_stats, 1)
                eng.wait_ge(hid_stats, 4 * s + 1)
                eng.tensor_tensor(hid_mean2[:, :], hid_mean[:, :], hid_mean[:, :], ALU.mult).then_inc(hid_stats, 1)
                eng.wait_ge(hid_stats, 4 * s + 2)
                eng.scalar_tensor_tensor(hid_var[:, :], ps[:, SQ_BANK, SQ_COL:SQ_COL + NT], 1.0 / HID, hid_mean2[:, :],
                                         ALU.mult, ALU.subtract).then_inc(hid_stats, 1)
                eng.wait_ge(hid_stats, 4 * s + 3)
                eng.tensor_scalar(hid_var_eps[:, :], hid_var[:, :], 0.0, LN_EPS, ALU.max, ALU.add).then_inc(hid_stats, 1)

            def hidden_out(s):
                eng.wait_ge(hid_rstd_ready, s + 1)
                for t in range(NT):
                    eng.scalar_tensor_tensor(mix[:, t, :], ps[:, 4 + t, 0:D], hid_rstd[:, t:t + 1], beta_row[:, :],
                                             ALU.mult, ALU.add).then_inc(y_ready, 1)
                for t in range(NT):
                    eng.wait_ge(y_hi_ready, 4 * s + t + 1)
                    low(node_lo[:, t, :], mix[:, t, :], node_hi[:, t, 0:D], y_lo_ready)

            def moments(n, stats, mean_sum, mean_gap, square_dev, gap_square, mean, factor, var_eps, stats_done, done):
                eng.wait_ge(stats_done, 4 * (n + 1))
                eng.tensor_tensor(mean_gap[:, :], stats[:, :, 1], stats[:, :, 4], ALU.subtract).then_inc(done, 1)
                eng.tensor_tensor(mean_sum[:, :], stats[:, :, 1], stats[:, :, 4], ALU.add).then_inc(done, 1)
                eng.scalar_tensor_tensor(square_dev[:, :], stats[:, :, 2], D * LN_EPS, stats[:, :, 5],
                                         ALU.add, ALU.add).then_inc(done, 1)
                eng.wait_ge(done, 6 * n + 1)
                eng.scalar_tensor_tensor(gap_square[:, :], mean_gap[:, :], 0.25, mean_gap[:, :],
                                         ALU.mult, ALU.mult).then_inc(done, 1)
                eng.wait_ge(done, 6 * n + 2)
                eng.tensor_scalar(mean[:, :], mean_sum[:, :], factor, None, ALU.mult).then_inc(done, 1)
                eng.wait_ge(done, 6 * n + 4)
                eng.scalar_tensor_tensor(var_eps[:, :], square_dev[:, :], 1.0 / D, gap_square[:, :],
                                         ALU.mult, ALU.add).then_inc(done, 1)

            def residual_sum(s):
                eng.wait_ge(resid_ready, 4 * (s + 1))
                for t in range(NT):
                    eng.wait_ge(scatter2_psum, 2 * s + t // 2 + 1)
                    eng.scalar_tensor_tensor(resid[:, t, :], half(4, t), Dn[:, t:t + 1], resid[:, t, :],
                                             ALU.mult, ALU.add).then_inc(sum_ready, 1)
                for t in range(NT):
                    eng.wait_ge(sum_ready, 4 * s + t + 1)
                    eng.bn_stats(stats0[:, t, :], resid[:, t, :]).then_inc(sum_stats, 1)
                moments(s, stats0, mean_sum0, mean_gap0, square_dev0, gap_square0, mean0, 0.5, var_eps0,
                        sum_stats, sum_moments)

            def normalise(s):
                eng.wait_ge(rstd0_ready, s + 1)
                wait(eng, X_copied, s)
                for t in range(NT):
                    eng.tensor_scalar(X[:, t, :], resid[:, t, :], mean0[:, t:t + 1], rstd0[:, t:t + 1],
                                      ALU.subtract, ALU.mult).then_inc(X_ready, 1)

            def XT_low(r):
                for d in range(DT):
                    eng.wait_ge(XT_hi_ready, 2 * r + d + 1)
                    low(XT_lo[:, d, :], ps[:, XT_BANKS[d], :], XT_hi[:, d, :], XT_lo_ready)

            def z2_low(r):
                eng.wait_ge(z2_psum, 4 * (r + 1))
                eng.tensor_copy(score_i[:, :], ps[:, 4:4 + NT, D + 2]).then_inc(score_i_ready, 1)
                wait(eng, exp_slope_ready, 4 * r)
                eng.tensor_scalar(bias_j[:, :], ps[:, 4:4 + NT, D], score_dots[:, 3:4], None,
                                  ALU.add).then_inc(bias_j_ready, 1)
                eng.tensor_scalar(bias_j_slope[:, :], ps[:, 4:4 + NT, D], score_dots[:, 3:4], SLOPE,
                                  ALU.add, ALU.mult).then_inc(bias_j_ready, 1)
                for t in range(NT):
                    eng.wait_ge(z2_hi_ready, 4 * r + t + 1)
                    low(z2_lo[:, t, :], ps[:, 4 + t, 0:D], z2_hi[:, t, 0:D], z2_lo_ready)

            def larger_exponential(r, j):
                eng.wait_ge(exp_ready, 4 * r + j + 1)
                eng.wait_ge(exp_slope_ready, 4 * r + j + 1)
                eng.tensor_tensor(expo[:, j, :], expo[:, j, :], expo_slope[:, j % 2, :],
                                  ALU.max).then_inc(exp_larger, 1)

            def attention_low(r, j):
                eng.wait_ge(att_hi_ready, 4 * r + j + 1)
                low(att_lo[:, j, :], expo[:, j, :], att_hi[:, j, :], att_lo_ready)

            def shift_z0(r, t):
                if not isinstance(r, int) or 0 < r < B - 1:
                    eng.wait_ge(out_ready, 4 * (r - 1) + t + 1)
                eng.wait_ge(z1_ready, 4 * r + t + 1)
                eng.tensor_tensor(z0_of(r)[:, t, :], ps[:, z10_banks(r)[t], D:2 * D], bk_row[:, :], ALU.add).then_inc(z0_ready, 1)

            def first_hop(r):
                eng.wait_ge(hop1_psum, 4 * (r + 1))
                eng.tensor_scalar(row_sum[:, :], ps[:, 0:NT, D], ROW_EPS, None, ALU.add).then_inc(rows_summed, 1)
                eng.wait_ge(rows_summed, r + 1)
                eng.reciprocal(row_inv[:, :], row_sum[:, :]).then_inc(row_inv_ready, 1)
                eng.wait_ge(row_inv_ready, r + 1)
                for t in range(NT):
                    eng.scalar_tensor_tensor(z1[:, t, :], ps[:, t, 0:D], row_inv[:, t:t + 1], z1[:, t, :],
                                             ALU.mult, ALU.add).then_inc(hop_ready, 1)
                for t in range(NT):
                    eng.wait_ge(hop_hi_ready, 4 * r + t + 1)
                    low(turn_lo[:, t * D:(t + 1) * D], z1[:, t, :], turn_hi[:, t * D:(t + 1) * D], hop_lo_ready)

            def last_hop_sum(r, tiles=range(NT)):
                for t in tiles:
                    eng.wait_ge(hop2_psum, 2 * r + t // 2 + 1)
                    eng.scalar_tensor_tensor(z0_of(r)[:, t, :], half(6, t), row_inv[:, t:t + 1], z0_of(r)[:, t, :],
                                             ALU.mult, ALU.add).then_inc(hop2_added, 1)

            def normalise_out(r, tiles):
                eng.wait_ge(shift1_ready, r + 1)
                wait(eng, out_stored, 16 * r)
                for t in tiles:
                    eng.tensor_scalar(out_sb[:, t, :], z0_of(r)[:, t, :], rstd1[:, t:t + 1], shift1[:, t:t + 1],
                                      ALU.mult, ALU.add).then_inc(out_ready, 1)

            def last_relu(r, tiles=slice(0, NT)):
                eng.wait_ge(hop2_added, 4 * r + tiles.stop)
                eng.wait_ge(X_copied, r + 1)
                eng.scalar_tensor_tensor(z0_of(r)[:, tiles, :], z0_of(r)[:, tiles, :], 0.0, X_kept[:, tiles, :],
                                         ALU.max, ALU.add).then_inc(relu_added, 1)

            def last_stats(r, tiles=range(NT), relus=1):
                eng.wait_ge(relu_added, r + relus)
                for t in tiles:
                    eng.bn_stats(stats1[:, t, :], z0_of(r)[:, t, :]).then_inc(out_stats, 1)

            def last_moments(r):
                moments(r, stats1, mean_sum1, mean_gap1, square_dev1, gap_square1, neg_mean1, -0.5, var_eps1,
                        out_stats, out_moments)

            def layer0():
                split_input(0)
                w1_low()
                transpose_incidence(0)
                widen_beta()
                edges(0)
                scale_w2()
                degrees(0)
                centre_w2()
                turn_low(0)
                split_w2()
                split_hidden(0)
                constant_dots()
                weight_dots(0)
                hidden_norm(0)
                hidden_out(0)
                weight_dots(1)
                split_dots()
                edges2(0)
                split_input(1)
                residual_sum(0)
                transpose_incidence(1)
                eng.wait_ge(dot_steps, DOT_STEPS)
                eng.wait_ge(wk_lo_ready, K)

            def body(r, last_hop, first_layer, prepare):
                s = r + 1
                normalise(r)
                if first_layer:
                    edges(s)
                if last_hop:
                    last_hop_sum(r - 1)
                XT_low(r)
                if last_hop:
                    last_relu(r - 1)
                if first_layer:
                    degrees(s)
                if last_hop:
                    if first_layer:
                        last_stats(r - 1)
                z2_low(r)
                if first_layer:
                    turn_low(s)
                larger_exponential(r, 0)
                if last_hop and first_layer:
                    last_moments(r - 1)
                for j in range(1, NT):
                    larger_exponential(r, j)
                if first_layer:
                    split_hidden(s)
                attention_low(r, 0)
                attention_low(r, 1)
                if not first_layer:
                    shift_z0(r, 0)
                    shift_z0(r, 1)
                attention_low(r, 2)
                attention_low(r, 3)
                for t in range(0 if first_layer else 2, NT):
                    shift_z0(r, t)
                if last_hop and not first_layer:
                    last_stats(r - 1)
                    last_moments(r - 1)
                if first_layer:
                    hidden_norm(s)
                    hidden_out(s)
                first_hop(r)
                if first_layer:
                    edges2(s)
                if prepare:
                    split_input(s + 1)
                if first_layer:
                    residual_sum(s)
                if prepare:
                    transpose_incidence(s + 1)

            def finish(r):
                for h in range(2):
                    last_hop_sum(r, range(2 * h, 2 * h + 2))
                    last_relu(r, slice(2 * h, 2 * h + 2))
                    last_stats(r, range(2 * h, 2 * h + 2), h + 1)
                eng.wait_ge(out_ready, 4 * r)
                last_moments(r)
                normalise_out(r, (2, 3))

            samples(eng, layer0, body, finish)

        @block.tensor
        def _(eng):
            def transpose_w1():
                eng.wait_ge(w1_loaded, 16)
                for d in range(DT):
                    for t in range(HT):
                        last = eng.transpose(ps[:, W1T_BANKS[d], tile(t)], w1_raw[:, t, tile(d)], ident[:, :])
                    last.then_inc(w1T_psum, 1)

            def transpose_w2():
                eng.wait_ge(w2_loaded, 16)
                for t in range(HT):
                    for d in range(DT):
                        last = eng.transpose(half(W2T_BANK, t)[:, tile(d)], w2_raw[:, d, tile(t)], ident[:, :])
                    last.then_inc(w2T_psum, 1)

            def sum_w2():
                eng.wait_ge(ones_wide_ready, 1)
                eng.wait_ge(w2_scaled, HT)
                for t in range(HT):
                    last = eng.matmul(ps[:, SUM_BANKS[0], 0:D], ones_wide, w2_gamma[:, t, :], start=(t == 0), stop=(t == HT - 1))
                last.then_inc(w2_sums_psum, 1)
                eng.wait_ge(beta_wide_ready, 1)
                for t in range(HT):
                    last = eng.matmul(ps[:, SUM_BANKS[1], 0:D], beta_wide[:, t, :], w2_plain[:, t, :], start=(t == 0), stop=(t == HT - 1))
                last.then_inc(w2_sums_psum, 1)

            def product(dst, terms, done=None, waits=()):
                for n, (stationary, moving) in enumerate(terms):
                    for term, semaphore, count in waits:
                        if term == n:
                            eng.wait_ge(semaphore, count)
                    width = moving.shape[-1]
                    last = eng.matmul(dst[:, 0:width], stationary, moving, start=(n == 0), stop=(n == len(terms) - 1))
                if done is not None:
                    last.then_inc(done, 1)

            def tile(t):
                return slice(t * P, (t + 1) * P)

            def transpose_adj(s, banks=T_BANKS):
                eng.wait_ge(adj_loaded, 16 * (s + 1))
                for t in range(NT):
                    if t >= 2:
                        wait(eng, hop_ready, 4 * (s - 2) + t - 1)
                    for c in range(NT):
                        last = eng.transpose(ps[:, banks[t], tile(c)], adj_sb[:, c, tile(t)], ident[:, :])
                    last.then_inc(adjT_psum, 1)

            def gather1(s):
                eng.wait_ge(inc_ready, s + 1)
                eng.wait_ge(x_hi_ready, s + 1)
                eng.wait_ge(adjT_ready, 4 * (s + 1))
                wait(eng, hop_ready, 4 * (s - 1))
                for t in range(NT):
                    product(ps[:, t, :], [(inc[:, c, tile(t)], node_hi[:, c, :]) for c in range(NT)]
                            + [(inc[:, c, tile(t)], node_lo[:, c, :]) for c in range(NT)], gather1_psum,
                            [(NT, x_lo_ready, s + 1)] if t == 0 else ())

            def scatter1(s):
                eng.wait_ge(incT_ready, s + 1)
                eng.wait_ge(w_ready, s + 1)
                eng.wait_ge(edge_lo_ready, 8 * s + 1)
                for t in range(NT):
                    product(ps[:, t, :], [(incT[:, e, tile(t)], edge_hi[:, e, :]) for e in range(NT)]
                            + [(incT[:, e, tile(t)], edge_lo[:, e, :]) for e in range(NT)], scatter1_psum,
                            [(e, edge_hi_ready, 8 * s + e + 1) for e in range(1, NT)]
                            + [(NT + e, edge_lo_ready, 8 * s + e + 1) for e in range(1, NT)] if t == 0 else ())

            def turn(s):
                for t in range(NT):
                    eng.wait_ge(mix_scaled, 4 * s + max(t + 1, DT))
                    for d in range(DT):
                        last = eng.transpose(ps[:, TURN_BANKS[d], tile(t)], mix[:, t, tile(d)], ident[:, :])
                        if t == NT - 1:
                            last.then_inc(turn_psum, 1)

            def hidden(s):
                wait(eng, z2_lo_ready, 4 * s)
                hi = [turn_hi[:, d * C:(d + 1) * C] for d in range(DT)]
                lo = [turn_lo[:, d * C:(d + 1) * C] for d in range(DT)]
                for t in range(HT):
                    product(ps[:, W1_BANKS[t], :], [(w1_hi[:, d, tile(t)], hi[d]) for d in range(DT)]
                            + [(w1_lo[:, d, tile(t)], hi[d]) for d in range(DT)]
                            + [(w1_hi[:, d, tile(t)], lo[d]) for d in range(DT)], hid_psum,
                            [(d, turn_hi_ready, 2 * s + d + 1) for d in range(DT)]
                            + [(2 * DT + d, turn_lo_ready, 2 * s + d + 1) for d in range(DT)] if t == 0 else ())

            def hidden_product(s):
                for t in range(NT):
                    product(ps[:, 4 + t, :], [(hid_hi[:, h, tile(t)], w2_hi[:, h, :]) for h in range(HT)]
                            + [(hid_hi[:, h, tile(t)], w2_lo[:, h, :]) for h in range(HT)]
                            + [(hid_lo[:, h, tile(t)], w2_hi[:, h, :]) for h in range(HT)], w2_psum,
                            [(h, hid_hi_ready, 4 * s + h + 1) for h in range(HT)]
                            + [(2 * HT + h, hid_lo_ready, 4 * s + h + 1) for h in range(HT)] if t == 0 else ())

            def sum_squares(s):
                eng.wait_ge(squares_added, 3 * (s + 1))
                for t in range(NT):
                    last = eng.matmul(ps[:, SQ_BANK, SQ_COL + t:SQ_COL + t + 1], square_sum[:, tile(t)], ones_col[:, :],
                                      start=True, stop=True)
                last.then_inc(square_psum, 1)

            def gather2(s):
                for t in range(NT):
                    product(half(4, t), [(inc[:, c, tile(t)], node_hi[:, c, 0:D]) for c in range(NT)]
                            + [(inc[:, c, tile(t)], node_lo[:, c, :]) for c in range(NT)],
                            gather2_psum if t % 2 else None,
                            [(c, y_hi_ready, 4 * s + c + 1) for c in range(NT)]
                            + [(NT + c, y_lo_ready, 4 * s + c + 1) for c in range(NT)] if t == 0 else ())

            def scatter2(s):
                eng.wait_ge(edge_lo_ready, 8 * s + 6)
                for t in range(NT):
                    product(half(4, t), [(incT[:, e, tile(t)], edge_hi[:, e, 0:D]) for e in range(NT)]
                            + [(incT[:, e, tile(t)], edge_lo[:, e, :]) for e in range(NT)],
                            scatter2_psum if t % 2 else None,
                            [(e, edge_hi_ready, 8 * s + 4 + e + 1) for e in range(2, NT)]
                            + [(NT + e, edge_lo_ready, 8 * s + 4 + e + 1) for e in range(2, NT)] if t == 0 else ())

            def transpose_X(r):
                eng.wait_ge(X_ready, 4 * (r + 1))
                for d in range(DT):
                    for t in range(NT):
                        last = eng.transpose(ps[:, XT_BANKS[d], tile(t)], X[:, t, tile(d)], ident[:, :])
                    last.then_inc(XT_psum, 1)

            def z2_product(r):
                eng.wait_ge(XT_lo_ready, 2 * r + 1)
                wait(eng, hop2_added, 4 * r)
                for t in range(NT):
                    product(ps[:, 4 + t, :], [(XT_hi[:, d, tile(t)], wk2_hi[:, d, :]) for d in range(DT)]
                            + [(XT_hi[:, d, tile(t)], wk2_lo[:, d, :]) for d in range(DT)]
                            + [(XT_lo[:, d, tile(t)], wk2_hi[:, d, :]) for d in range(DT)], z2_psum,
                            [(1, XT_hi_ready, 2 * r + 2), (2 * DT + 1, XT_lo_ready, 2 * r + 2)] if t == 0 else ())

            def spread_scores(r, first_layer):
                if first_layer:
                    eng.wait_ge(mix_scaled, 4 * (r + 2))
                else:
                    eng.wait_ge(hop_ready, 4 * r)
                eng.wait_ge(score_i_ready, r + 1)
                for t in range(NT):
                    last = eng.transpose(ps[:, SI_BANK, tile(t)], score_i[:, t:t + 1].to_broadcast([P, P]), ident[:, :])
                last.then_inc(si_psum, 1)

            def z10_product(r, t):
                if z10_banks(r)[t] == SI_BANK:
                    eng.wait_ge(exp_slope_ready, 4 * (r + 1))
                if z10_banks(r)[t] == 4:
                    eng.wait_ge(z2_lo_ready, 4 * r + 1)
                product(ps[:, z10_banks(r)[t], :], [(XT_hi[:, d, tile(t)], wk10_hi[:, d, :]) for d in range(DT)]
                        + [(XT_lo[:, d, tile(t)], wk10_hi[:, d, :]) for d in range(DT)]
                        + [(XT_hi[:, d, tile(t)], wk10_lo[:, d, :]) for d in range(DT)], z10_psum)

            def first_hop(r):
                eng.wait_ge(z2_lo_ready, 4 * (r + 1))
                for t in range(NT):
                    if t in z10_banks(r):
                        eng.wait_ge(z0_ready, 4 * r + z10_banks(r).index(t) + 1)
                    else:
                        eng.wait_ge(exp_slope_ready, 4 * (r + 1))
                    product(ps[:, t, :], [(att_hi[:, j, tile(t)], z2_hi[:, j, :]) for j in range(NT)]
                            + [(att_hi[:, j, tile(t)], z2_lo[:, j, :]) for j in range(NT)]
                            + [(att_lo[:, j, tile(t)], z2_hi[:, j, :]) for j in range(NT)], hop1_psum,
                            [(j, att_hi_ready, 4 * r + j + 1) for j in range(NT)]
                            + [(2 * NT + j, att_lo_ready, 4 * r + j + 1) for j in range(NT)] if t == 0 else ())

            def last_hop_product(r):
                eng.wait_ge(adjT_ready, min(4 * (r + 3), 4 * B) if isinstance(r, int) else 4 * (r + 3))
                hi = [turn_hi[:, j * D:(j + 1) * D] for j in range(NT)]
                lo = [turn_lo[:, j * D:(j + 1) * D] for j in range(NT)]
                for t in range(NT):
                    product(half(6, t), [(att_hi[:, j, tile(t)], hi[j]) for j in range(NT)]
                            + [(att_lo[:, j, tile(t)], hi[j]) for j in range(NT)]
                            + [(att_hi[:, j, tile(t)], lo[j]) for j in range(NT)],
                            hop2_psum if t % 2 else None,
                            [(j, hop_hi_ready, 4 * r + j + 1) for j in range(NT)]
                            + [(2 * NT + j, hop_lo_ready, 4 * r + j + 1) for j in range(NT)] if t == 0 else ())

            def layer0():
                eng.wait_ge(ident_ready, 2)
                eng.wait_ge(ones_ready, 4)
                transpose_adj(0)
                transpose_w1()
                gather1(0)
                transpose_w2()
                scatter1(0)
                eng.wait_ge(w1_lo_ready, DT)
                sum_w2()
                turn(0)
                eng.wait_ge(w2_centred, HT + 1)
                hidden(0)
                eng.wait_ge(w2_split, 2)
                hidden_product(0)
                sum_squares(0)
                transpose_adj(1, T1_BANKS)
                gather2(0)
                scatter2(0)
                eng.wait_ge(wk_lo_ready, K)
                eng.wait_ge(dot_steps, DOT_STEPS)

            def body(r, last_hop, first_layer, prepare):
                s = r + 1
                if first_layer:
                    gather1(s)
                if last_hop:
                    last_hop_product(r - 1)
                transpose_X(r)
                if first_layer:
                    scatter1(s)
                z2_product(r)
                if first_layer:
                    turn(s)
                spread_scores(r, first_layer)
                z10_product(r, 0)
                if first_layer:
                    hidden(s)
                for t in range(1, NT):
                    z10_product(r, t)
                if first_layer:
                    hidden_product(s)
                    sum_squares(s)
                first_hop(r)
                if first_layer:
                    gather2(s)
                if prepare:
                    transpose_adj(s + 1)
                if first_layer:
                    scatter2(s)

            samples(eng, layer0, body, last_hop_product)


_INS = ['x', 'adj', 'L0_gnn_W1', 'L0_gnn_b1', 'L0_gnn_gamma', 'L0_gnn_beta', 'L0_gnn_W2', 'L0_gnn_b2',
        'L1_gnn_Wv', 'L1_gnn_bv', 'L1_gnn_aw', 'L1_gnn_ab', 'L1_gnn_Wk', 'L1_gnn_bk']
_OUTS = [((16, 512, 256), 'float32')]


def kernel(**inputs):
    import numpy as _np
    import concourse.bacc as _bacc
    from concourse import mybir as _mybir
    from concourse.bass_utils import run_bass_kernel_spmd as _run

    nc = _bacc.Bacc("TRN2", target_bir_lowering=False, num_devices=1)
    arrays, args = {}, []
    for name in _INS:
        a = _np.ascontiguousarray(inputs[name])
        arrays[f"in_{name}_dram"] = a
        args.append(nc.dram_tensor(f"in_{name}_dram", a.shape, _mybir.dt.from_np(a.dtype), kind="ExternalInput").ap())
    for i, (shape, dtype) in enumerate(_OUTS):
        dt = _mybir.dt.from_np(_np.dtype(dtype))
        args.append(nc.dram_tensor(f"out_{i}_dram", shape, dt, kind="ExternalOutput").ap())
    resnorm_hypergraph_attention_kernel(nc, *args)
    r = _run(nc, [arrays], core_ids=[0])
    got = tuple(r.results[0][f"out_{i}_dram"] for i in range(len(_OUTS)))
    return got[0]
```
